# Optimizing a Trainium2 kernel written in Bass

```python
import numpy as np
import jax
import jax.numpy as jnp

def _softmax(x, axis=-1):
    return jax.nn.softmax(x, axis=axis)

def _gelu(x):
    return jax.nn.gelu(x, approximate=True)

def _silu(x):
    return jax.nn.silu(x)

def _sigmoid(x):
    return jax.nn.sigmoid(x)

def _layernorm(x, axis=-1, eps=1e-05):
    m = jnp.mean(x, axis=axis, keepdims=True)
    v = jnp.var(x, axis=axis, keepdims=True)
    return (x - m) / jnp.sqrt(v + eps)

def _scatter_add(tgt, idx, src, axis=0):
    return tgt.at[idx].add(src)

def _segment_sum(src, seg, n):
    return jax.ops.segment_sum(src, seg, n)
kernel_name = 'mk_cond_resid_d4_seqx_r4_aca9e0'

def setup_inputs(seed: int=0):
    np.random.seed(seed)
    _w = jnp.asarray

    def _rec_inputs():
        import jax
        import jax.numpy as jnp
        _rk = jax.random.key(seed)
        x = -7.109e-05 + 0.9999 * jax.random.normal(jax.random.fold_in(_rk, 1), (64, 64, 512), jnp.float32)
        _lenS = 64 - jax.random.randint(jax.random.fold_in(_rk, 7), (64,), 0, max(1, 64 // 4) + 1, jnp.int32)
        _lenS2 = 64 - jax.random.randint(jax.random.fold_in(_rk, 8), (64,), 0, max(1, 64 // 4) + 1, jnp.int32)
        itok_B_1_198 = jax.random.randint(jax.random.fold_in(_rk, 11), (64,), 1, 199, jnp.int32)
        itok_B_0_7 = jax.random.randint(jax.random.fold_in(_rk, 12), (64,), 0, 8, jnp.int32)
        fside_8xS_0 = -0.00162727 + 0.0609077 * jax.random.normal(jax.random.fold_in(_rk, 13), (8, 64), jnp.float32)
        return (x, itok_B_1_198, itok_B_0_7, fside_8xS_0)
    x, itok_B_1_198, itok_B_0_7, fside_8xS_0 = _rec_inputs()

    def _L0_cond_setup():
        import jax, jax.numpy as jnp
        import numpy as np
        B, C, T = (128, 64, 512)
        S, D = (200, 64)
        key = jax.random.key(seed)
        k1, k2, k3 = jax.random.split(key, 3)
        x = jax.random.normal(k1, (B, C, T), dtype=jnp.float32)
        conditions = jax.random.randint(k2, (B,), 0, S, dtype=jnp.int64)
        weights = jax.random.normal(k3, (S, C, D), dtype=jnp.float32) / jnp.sqrt(jnp.float32(C))
        return {'x': x, 'conditions': conditions, 'weights': weights}
    _L0_cond_all = _L0_cond_setup()
    _L0_cond_in = {k: v for k, v in _L0_cond_all.items() if k in ('weights',)}
    del _L0_cond_all

    def _L1_cond_setup():
        import jax, jax.numpy as jnp
        import numpy as np
        B, C, D, T, N_SUBJECTS = (128, 64, 64, 512, 8)
        key = jax.random.key(seed)
        kx, ks, kw = jax.random.split(key, 3)
        x = jax.random.normal(kx, (B, C, T), dtype=jnp.float32)
        subjects = jax.random.randint(ks, (B,), 0, N_SUBJECTS, dtype=jnp.int64)
        weights = jax.random.normal(kw, (N_SUBJECTS, C, D), dtype=jnp.float32) * (1.0 / C ** 0.5)
        return {'x': x, 'subjects': subjects, 'weights': weights}
    _L1_cond_all = _L1_cond_setup()
    _L1_cond_in = {k: v for k, v in _L1_cond_all.items() if k in ('weights',)}
    del _L1_cond_all

    def _L2_cond_setup():
        import jax, jax.numpy as jnp
        import numpy as np
        B, C, T = (64, 64, 512)
        D, N = (64, 8)
        key = jax.random.key(seed)
        k_x, k_s, k_w, k_b = jax.random.split(key, 4)
        scale = 1.0 / np.sqrt(C)
        x = jax.random.normal(k_x, (B, C, T), dtype=jnp.float32)
        subjects = jax.random.randint(k_s, (B,), 0, N, dtype=jnp.int64)
        weights = jax.random.normal(k_w, (N, C, D), dtype=jnp.float32) * scale
        bias = jax.random.normal(k_b, (N, D), dtype=jnp.float32) * scale
        return {'x': x, 'subjects': subjects, 'weights': weights, 'bias': bias}
    _L2_cond_all = _L2_cond_setup()
    _L2_cond_in = {k: v for k, v in _L2_cond_all.items() if k in ('weights',)}
    del _L2_cond_all

    def _L3_cond_setup():
        import jax, jax.numpy as jnp
        import numpy as np

        def _lora_linear(x, W, A, B, adapter_indices):
            base = jnp.einsum('bsd,df->bsf', x, W)
            Ai = A[adapter_indices]
            Bi = B[adapter_indices]
            lora = jnp.einsum('bsr,brf->bsf', jnp.einsum('bsd,bdr->bsr', x, Ai), Bi)
            return base + lora
        key = jax.random.key(seed)
        ks = jax.random.split(key, 10)
        H, I, N, R = (512, 2048, 8, 16)
        B, S = (4, 512)
        std_h = 1.0 / np.sqrt(H)
        std_i = 1.0 / np.sqrt(I)
        x = jax.random.normal(ks[0], (B, S, H), dtype=jnp.float32)
        adapter_indices = jax.random.randint(ks[1], (B,), 0, N, dtype=jnp.int32)
        Wg = jax.random.normal(ks[2], (H, I), dtype=jnp.float32) * std_h
        Wu = jax.random.normal(ks[3], (H, I), dtype=jnp.float32) * std_h
        Wd = jax.random.normal(ks[4], (I, H), dtype=jnp.float32) * std_i
        Ag = jax.random.normal(ks[5], (N, H, R), dtype=jnp.float32) * std_h
        Bg = jnp.zeros((N, R, I), dtype=jnp.float32) + 0.01
        Au = jax.random.normal(ks[6], (N, H, R), dtype=jnp.float32) * std_h
        Bu = jnp.zeros((N, R, I), dtype=jnp.float32) + 0.01
        Ad = jax.random.normal(ks[7], (N, I, R), dtype=jnp.float32) * std_i
        Bd = jnp.zeros((N, R, H), dtype=jnp.float32) + 0.01
        return {'x': x, 'Wg': Wg, 'Wu': Wu, 'Wd': Wd, 'Ag': Ag, 'Bg': Bg, 'Au': Au, 'Bu': Bu, 'Ad': Ad, 'Bd': Bd, 'adapter_indices': adapter_indices}
    _L3_cond_all = _L3_cond_setup()
    _L3_cond_in = {k: v for k, v in _L3_cond_all.items() if k in ('Wg', 'Wu', 'Wd', 'Ag', 'Bg', 'Au', 'Bu', 'Ad', 'Bd')}
    del _L3_cond_all
    return {'x': x, 'itok_B_1_198': itok_B_1_198, 'itok_B_0_7': itok_B_0_7, 'fside_8xS_0': fside_8xS_0, 'L0_cond_weights': _L0_cond_in['weights'], 'L1_cond_weights': _L1_cond_in['weights'], 'L2_cond_weights': _L2_cond_in['weights'], 'L3_cond_Wg': _L3_cond_in['Wg'], 'L3_cond_Wu': _L3_cond_in['Wu'], 'L3_cond_Wd': _L3_cond_in['Wd'], 'L3_cond_Ag': _L3_cond_in['Ag'], 'L3_cond_Bg': _L3_cond_in['Bg'], 'L3_cond_Au': _L3_cond_in['Au'], 'L3_cond_Bu': _L3_cond_in['Bu'], 'L3_cond_Ad': _L3_cond_in['Ad'], 'L3_cond_Bd': _L3_cond_in['Bd']}

def reference(x, itok_B_1_198, itok_B_0_7, fside_8xS_0, L0_cond_weights, L1_cond_weights, L2_cond_weights, L3_cond_Wg, L3_cond_Wu, L3_cond_Wd, L3_cond_Ag, L3_cond_Bg, L3_cond_Au, L3_cond_Bu, L3_cond_Ad, L3_cond_Bd):
    import jax
    import jax.numpy as jnp

    def _L0_cond_ref(x, conditions, weights):
        import jax, jax.numpy as jnp
        import numpy as np
        B, C, T = (128, 64, 512)
        S, D = (200, 64)
        w = weights[conditions]
        return jnp.einsum('bct,bcd->bdt', x, w)

    def _L1_cond_ref(x, subjects, weights):
        import jax, jax.numpy as jnp
        import numpy as np
        B, C, D, T, N_SUBJECTS = (128, 64, 64, 512, 8)
        w = weights[subjects]
        out = jnp.einsum('bct,bcd->bdt', x, w)
        return out

    def _L2_cond_ref(x, subjects, weights, bias):
        import jax, jax.numpy as jnp
        import numpy as np
        B, C, T = (64, 64, 512)
        D, N = (64, 8)
        w = weights[subjects]
        b = bias[subjects]
        out = jnp.einsum('bct,bcd->bdt', x, w)
        out = out + b[:, :, None]
        return out

    def _L3_cond_ref(x, Wg, Wu, Wd, Ag, Bg, Au, Bu, Ad, Bd, adapter_indices):
        import jax, jax.numpy as jnp
        import numpy as np

        def _lora_linear(x, W, A, B, adapter_indices):
            base = jnp.einsum('bsd,df->bsf', x, W)
            Ai = A[adapter_indices]
            Bi = B[adapter_indices]
            lora = jnp.einsum('bsr,brf->bsf', jnp.einsum('bsd,bdr->bsr', x, Ai), Bi)
            return base + lora
        gate = _lora_linear(x, Wg, Ag, Bg, adapter_indices)
        up = _lora_linear(x, Wu, Au, Bu, adapter_indices)
        h = jax.nn.silu(gate) * up
        return _lora_linear(h, Wd, Ad, Bd, adapter_indices)
    x = x + _L0_cond_ref(x, itok_B_1_198, L0_cond_weights)
    x = x + _L1_cond_ref(x, itok_B_0_7, L1_cond_weights)
    x = x + _L2_cond_ref(x, itok_B_0_7, L2_cond_weights, fside_8xS_0)
    x = x + _L3_cond_ref(x, L3_cond_Wg, L3_cond_Wu, L3_cond_Wd, L3_cond_Ag, L3_cond_Bg, L3_cond_Au, L3_cond_Bu, L3_cond_Ad, L3_cond_Bd, itok_B_0_7)
    return x

_drawn_inputs = setup_inputs


def setup_inputs(seed=0):
    import zlib

    import numpy as np

    out = dict(_drawn_inputs(seed))
    spreads = {'L3_cond_Bg': (0.009999999776482582, 0.6),
     'L3_cond_Bu': (0.009999999776482582, 0.6),
     'L3_cond_Bd': (0.009999999776482582, 0.6)}
    factors = {}
    for name, (base, spread) in spreads.items():
        noise = np.random.default_rng([zlib.crc32(name.encode()), seed]).standard_normal(out[name].shape)
        drawn = base * np.exp(spread * noise) if base else spread * noise
        out[name] = jnp.asarray(drawn.astype(out[name].dtype))
    for name, factor in factors.items():
        out[name] = (out[name] * factor).astype(out[name].dtype)
    return out
```

```python
from contextlib import ExitStack

import concourse.bass as bass
from concourse import mybir

F32 = mybir.dt.float32
F32R = mybir.dt.float32r
I32 = mybir.dt.int32
U32 = mybir.dt.uint32
ALU = mybir.AluOpType
ACT = mybir.ActivationFunctionType

P = 128
SAMPLES, C, T = 64, 64, 512
ADAPTERS, RANK = 8, 16
HIDDEN = 2048
KC = T // P
BLOCKS = HIDDEN // P
PAIRS = SAMPLES // 2
HALVES = 2
HPAIRS = PAIRS // HALVES
TP = 4
TILES = HPAIRS // TP
TOK = TP * P
STEPS = BLOCKS * TILES
BODY = 2 * TILES
TURNS = STEPS // BODY
LAYERS = 3

CHUNKS = ((0, 512), (512, 1024), (1024, 1536), (1536, 1664))
WCOLS = CHUNKS[-1][1]
GATE, UP, DOWN, ADOWN = (lo for lo, _ in CHUNKS)
NCH = len(CHUNKS)
ACH = 2
CONV = ACH + NCH * BLOCKS
DB = TP + 1
BCH = 4
BCOLS = BLOCKS * 2 * P // BCH


def cond_resid_kernel(nc, x, subject, adapter, w0_rows, w12_rows, bias_t, w_all, a_all, b_rows, bd_rows, out):
    b_table = nc.dram_tensor("b_table", (2 * P * BLOCKS, 2 * P), F32).ap()
    x3_next = nc.dram_tensor("x3_next", (HPAIRS, P, T), F32).ap()

    with ExitStack() as ctx:
        def sb(name, shape, dt=F32):
            return ctx.enter_context(nc.sbuf_tensor(name, shape, dt))

        def bank(name):
            return ctx.enter_context(nc.psum_tensor(name, [P, 512], F32))

        def sem(name):
            return ctx.enter_context(nc.semaphore(name))

        xt_hi = sb("xt_hi", [P, KC, TILES * TOK], F32R)
        xt_lo = sb("xt_lo", [P, KC, TILES * TOK], F32R)
        acc = sb("acc", [P, HPAIRS, T])
        u = sb("u", [P, 2, TILES * TOK], F32R)
        vacc = sb("vacc", [P, TILES * TOK])
        w_raw = sb("w_raw", [P, WCOLS])
        w_hi = sb("w_hi", [P, 2, WCOLS], F32R)
        w_lo = sb("w_lo", [P, 2, WCOLS], F32R)
        b_got = sb("b_got", [P, 2, TP, 2 * P], F32R)
        silu = sb("silu", [P, TOK])
        h = sb("h", [P, TOK])
        h_hi = sb("h_hi", [P, 2, TOK], F32R)
        h_lo = sb("h_lo", [P, 2, TOK], F32R)
        xn = sb("xn", [P, 2, T])
        xn_hi = sb("xn_hi", [P, T], F32R)
        xn_lo = sb("xn_lo", [P, T], F32R)
        bd_hi = sb("bd_hi", [P, LAYERS, TP, P], F32R)
        bd_lo = sb("bd_lo", [P, LAYERS, TP, P], F32R)
        bd_raw = sb("bd_raw", [P, LAYERS, TP, C])
        bdn_hi = sb("bdn_hi", [P, T], F32R)
        bdn_lo = sb("bdn_lo", [P, T], F32R)
        ident = sb("ident", [P, P])
        pattern = sb("pattern", [P, 2, 4 * RANK])
        sel = sb("sel", [P, 2, 2, 2, 4 * RANK], F32R)
        ints = sb("ints", [P, 2, SAMPLES], I32)
        adf = sb("adf", [P, SAMPLES])
        pair_ad = sb("pair_ad", [P, PAIRS])
        pair_su = sb("pair_su", [P, PAIRS])
        onehot = sb("onehot", [P, SAMPLES])
        bias = sb("bias", [P, PAIRS])
        bias_n = sb("bias_n", [P, PAIRS])
        bias_src = sb("bias_src", [P, ADAPTERS])
        p_int = sb("p_int", [P, 8], I32)
        p_f = sb("p_f", [P, 4])
        half_mask = sb("half_mask", [P, 2])
        r_int = sb("r_int", [P, RANK], I32)
        r_int2 = sb("r_int2", [P, RANK], I32)
        idx_w = sb("idx_w", [P, PAIRS, 2], I32)
        idx_b0 = sb("idx_b0", [P, PAIRS], I32)
        idx_b = sb("idx_b", [P, 2, PAIRS], I32)
        idx_now = sb("idx_now", [P, 2, 2], I32)

        pg = [bank(f"pg{i}") for i in range(2)]
        pu = [bank(f"pu{i}") for i in range(2)]
        pd = [bank(f"pd{i}") for i in range(2)]
        pv = bank("pv")
        px = bank("px")
        layer_bank = [px, pv, pd[0], pd[1]]

        ints_in = sem("ints_in")
        x_in = [sem(f"x_in{t}") for t in range(TILES)]
        b_in = [sem(f"b_in{i}") for i in range(2)]
        bdn_in = sem("bdn_in")
        raw_in = [sem(f"raw_in{c}") for c in range(NCH)]
        b_out = [sem(f"b_out{i}") for i in range(2)]
        x3_out = [sem(f"x3_out{i}") for i in range(2)]
        x3_in = [sem(f"x3_in{t}") for t in range(TILES)]
        xn_in = [sem(f"xn_in{i}") for i in range(2)]
        y_out = [sem(f"y_out{t}") for t in range(TILES)]
        bd_in = [sem(f"bd_in{i}") for i in range(TP)]
        b_got_in = [sem(f"b_got_in{i}") for i in range(2)]
        consts = sem("consts")
        pool_step = sem("pool_step")
        dve_step = sem("dve_step")
        idx_done = sem("idx_done")
        b_hi_done = sem("b_hi_done")
        b_lo_done = sem("b_lo_done")
        bdn_done = sem("bdn_done")
        bdn_hi_done = sem("bdn_hi_done")
        bd_hi_done = sem("bd_hi_done")
        bd_lo_done = sem("bd_lo_done")
        lx_hi = sem("lx_hi")
        lx_lo_p = sem("lx_lo_p")
        lx_lo_v = sem("lx_lo_v")
        layer_mm = sem("layer_mm")
        layer_add = sem("layer_add")
        tr_mm = sem("tr_mm")
        xt_hi_done = sem("xt_hi_done")
        xt_done = sem("xt_done")
        a_mm = sem("a_mm")
        ua_hi = sem("ua_hi")
        ua_done = sem("ua_done")
        sel_done = sem("sel_done")
        sel_mm = sem("sel_mm")
        u_done = sem("u_done")
        v_zero = sem("v_zero")
        w_hi_done = sem("w_hi_done")
        w_done = sem("w_done")
        gate_mm = sem("gate_mm")
        up_mm = sem("up_mm")
        silu_done = sem("silu_done")
        h_done = sem("h_done")
        h_hi_done = sem("h_hi_done")
        h_lo_done = sem("h_lo_done")
        down_mm = sem("down_mm")
        down_add = sem("down_add")
        v_masked = sem("v_masked")
        v_hi_done = sem("v_hi_done")
        v_done = sem("v_done")
        bdown_mm = sem("bdown_mm")
        y_add = sem("y_add")
        idx_next = sem("idx_next")
        may_gather = sem("may_gather")

        block = ctx.enter_context(nc.Block())

        def conv(half, blk, c):
            return CONV * half + (c + 1 if isinstance(blk, int) and blk < 0 else blk * NCH + (ACH + c + 1))

        def raw_loads(half, blk, c):
            per = BLOCKS + (1 if c < ACH else 0)
            return per * half + (1 if isinstance(blk, int) and blk < 0 else blk + (2 if c < ACH else 1))

        def silus(n): return n + 1
        def hs(n): return n + 1
        def downs(n): return n + 1
        def adds(n): return n + 1

        def layer_no(q, l):
            if isinstance(q, int) and q < HPAIRS:
                return (q // TP) * TP * LAYERS + l * TP + q % TP + 1
            return q * LAYERS + (l + 1)

        def lo_no(q, l):
            if isinstance(q, int) and q < HPAIRS:
                return (q // TP) * 2 * LAYERS + l * 2 + (q % TP) // 2 + 1
            return HPAIRS // 2 * LAYERS + (q - HPAIRS) * LAYERS + (l + 1)

        def layer_in(q_slot, first_half):
            if first_half:
                tail = slice((TILES - 1) * TOK, TILES * TOK)
                return xt_hi[:, q_slot, tail], xt_lo[:, q_slot, tail]
            return xn_hi[:, :], xn_lo[:, :]

        def start_order():
            yield "layers", 0
            for t in range(TILES):
                if t + 1 < TILES:
                    yield "layers", t + 1
                yield "tile", t

        @block.sync
        def _(sp):
            def load_raw(half, blk, c):
                lo, hi = CHUNKS[c]
                if isinstance(blk, int) and blk < 0:
                    src = a_all[:, lo:hi]
                elif isinstance(blk, int):
                    src = w_all[blk, :, lo:hi]
                else:
                    src = w_all[bass.ds(blk, 1), :, lo:hi].rearrange("a p n -> (a p) n")
                sp.dma_start(w_raw[:, lo:hi], src).then_inc(raw_in[c], 16)

            def load_x(t):
                src = x[2 * TP * t:2 * TP * (t + 1)].rearrange("(q s) c t -> (s c) q t", s=2)
                sp.dma_start(acc[:, TP * t:TP * (t + 1), :], src).then_inc(x_in[t], 16)

            def load_b(j):
                if j >= 2:
                    sp.wait_ge(b_lo_done, j - 1)
                sp.dma_start(vacc[:, (j % 2) * BCOLS:(j % 2 + 1) * BCOLS],
                             b_rows[:, j * BCOLS:(j + 1) * BCOLS]).then_inc(b_in[j % 2], 16)

            def store_b(j):
                sp.wait_ge(b_lo_done, j + 1)
                table = b_table.rearrange("(g p k) n -> g p (k n)", g=2, k=BLOCKS)
                for part in range(2):
                    sp.dma_start(table[part, :, j * BCOLS:(j + 1) * BCOLS],
                                 u[:, part, (j % 2) * BCOLS:(j % 2 + 1) * BCOLS].bitcast(F32)
                                 ).then_inc(b_out[j % 2], 16)

            def load_xn(q, slot):
                src = (x[2 * q:2 * q + 2] if isinstance(q, int) else x[bass.ds(q * 2, 2)])
                sp.dma_start(xn[:, slot, :], src.rearrange("s c t -> (s c) t")).then_inc(xn_in[slot], 16)

            sp.dma_start(ints[:, 0, :], subject.partition_broadcast(P)).then_inc(ints_in, 16)
            sp.dma_start(ints[:, 1, :], adapter.partition_broadcast(P)).then_inc(ints_in, 16)
            for s in range(2):
                sp.dma_start(bias_src[s * C:(s + 1) * C, :], bias_t).then_inc(ints_in, 16)
            load_x(0)
            load_b(0)
            load_b(1)
            load_x(1)
            load_raw(0, -1, 0)
            load_raw(0, -1, 1)
            sp.dma_start(silu[:, :], bd_rows).then_inc(bdn_in, 16)
            store_b(0)
            load_b(2)
            load_x(2)
            store_b(1)
            load_b(3)
            load_x(3)
            load_xn(HPAIRS, 0)
            load_xn(HPAIRS + 1, 1)
            store_b(2)
            store_b(3)

            def half_start(half):
                for c in range(NCH):
                    if c < ACH:
                        sp.wait_ge(w_done, conv(half, -1, c))
                    load_raw(half, 0, c)
                for c in range(NCH):
                    sp.wait_ge(w_done, conv(half, 0, c))
                    load_raw(half, 1, c)

            def body(half, i, last):
                for k in range(BODY):
                    blk = i * 2 + (k // TILES)
                    c = k % TILES
                    if not (last and k // TILES == 1):
                        if not last:
                            sp.wait_ge(w_done, conv(half, blk + 1, c))
                            load_raw(half, blk + 2, c)
                        elif half + 1 < HALVES and c < ACH:
                            sp.wait_ge(w_done, conv(half, blk + 1, c))
                            load_raw(half + 1, -1, c)
                    if half == 0 and c == 2:
                        slot = k // TILES
                        q = HPAIRS + blk
                        sp.wait_ge(layer_add, layer_no(q, 2))
                        if isinstance(blk, int):
                            dst = x3_next[blk]
                        else:
                            dst = x3_next[bass.ds(blk, 1)].rearrange("a p t -> (a p) t")
                        sp.dma_start(dst, xn[:, slot, :]).then_inc(x3_out[slot], 16)
                        if not last:
                            sp.wait_ge(x3_out[slot], i * 16 + 16)
                            load_xn(q + 2, slot)

            for half in range(HALVES):
                half_start(half)
                with sp.Fori(0, TURNS - 1) as i:
                    body(half, i, False)
                body(half, TURNS - 1, True)
                if half == 0:
                    for s in range(2):
                        sp.wait_ge(x3_out[s], TURNS * 16)
                for t in range(TILES):
                    first = 2 * TP * (half * TILES + t)
                    sp.wait_ge(y_add, half * HPAIRS + TP * (t + 1))
                    sp.dma_start(out[first:first + 2 * TP].rearrange("(q s) c t -> (s c) q t", s=2),
                                 acc[:, TP * t:TP * (t + 1), :]).then_inc(y_out[t], 16)
                if half == 0:
                    for t in range(TILES):
                        sp.wait_ge(y_out[t], 16)
                        sp.dma_start(acc[:, TP * t:TP * (t + 1), :],
                                     x3_next[TP * t:TP * (t + 1)].rearrange("q p t -> p q t")
                                     ).then_inc(x3_in[t], 16)
            for t in range(TILES):
                sp.wait_ge(y_out[t], 32)
            for s in range(2):
                sp.wait_ge(b_out[s], 4 * 16)

        @block.gpsimd
        def _(gp):
            chain = [0]

            def link(ins):
                chain[0] += 1
                ins.then_inc(pool_step, 1)
                gp.wait_ge(pool_step, chain[0])

            link(gp.iota(p_int[:, 0:1], [[0, 1]], base=0, channel_multiplier=1))
            gp.memset(ident[:, :], 0.0).then_inc(pool_step, 1)
            gp.iota(r_int[:, :], [[1, RANK]], base=P, channel_multiplier=-1).then_inc(consts, 1)
            chain[0] += 1
            gp.wait_ge(pool_step, chain[0])
            gp.affine_select(out=ident[:, :], in_=ident[:, :], compare_op=ALU.not_equal, fill=1.0, base=0,
                             pattern=[[-1, P]], channel_multiplier=1).then_inc(consts, 1)
            gp.memset(bd_hi[:, :, :, :].bitcast(F32), 0.0).then_inc(consts, 1)
            gp.memset(bd_lo[:, :, :, :].bitcast(F32), 0.0).then_inc(consts, 1)
            gp.wait_ge(idx_done, 1)

            def wait_before_gather(semaphore, value):
                gp.wait_ge(semaphore, value)
                gp.sem_inc(may_gather, 1)

            def gather_w(q, slot, now=None):
                i0 = idx_w[:, q, 0:1] if now is None else idx_now[:, now, 0:1]
                i1 = idx_w[:, q, 1:2] if now is None else idx_now[:, now, 1:2]
                gp.indirect_dma_start(out=bd_raw[:, 0, slot, :], out_offset=None, in_=w0_rows,
                                      in_offset=bass.IndirectOffsetOnAxis(ap=i0.bitcast(U32), axis=0)
                                      ).then_inc(bd_in[slot], 16)
                for l in range(2):
                    gp.indirect_dma_start(out=bd_raw[:, 1 + l, slot, :], out_offset=None, in_=w12_rows[l],
                                          in_offset=bass.IndirectOffsetOnAxis(ap=i1.bitcast(U32), axis=0)
                                          ).then_inc(bd_in[slot], 16)

            def gather_b(half, n, s, parity, slot):
                for j in range(TP):
                    q = half * HPAIRS + s * TP + j
                    gp.indirect_dma_start(
                        out=b_got[:, slot, j, :].bitcast(F32), out_offset=None, in_=b_table,
                        in_offset=bass.IndirectOffsetOnAxis(ap=idx_b[:, parity, q:q + 1].bitcast(U32), axis=0)
                    ).then_inc(b_got_in[slot], 16)

            def layer_lo(q, l, source, slot, first_half):
                hi, lo = layer_in(slot, first_half)
                gp.wait_ge(lx_hi, layer_no(q, l))
                gp.tensor_tensor(lo, source, hi, ALU.subtract).then_inc(lx_lo_p, 1)

            def next_block(half, parity, turn_no):
                gp.tensor_scalar(idx_b[:, parity, :], idx_b[:, 1 - parity, :], 1.0, None, ALU.add
                                 ).then_inc(idx_next, 1)
                wait_before_gather(idx_next, turn_no)

            for q in range(TP):
                gather_w(q, q)
            for kind, t in start_order():
                if kind == "layers":
                    for l in range(LAYERS):
                        for j in (1, 3):
                            q = t * TP + j
                            if l:
                                gp.wait_ge(layer_add, layer_no(q, l - 1))
                            layer_lo(q, l, acc[:, q, :], j, True)
                    if t + 1 < TILES:
                        for j in range(TP):
                            q = (t + 1) * TP + j
                            gp.wait_ge(bd_lo_done, q - TP + 1)
                            gather_w(q, j)
            gp.wait_ge(bd_lo_done, HPAIRS - TP + 1)
            gather_w(HPAIRS, 0)

            def half_start(half):
                if half == 0:
                    for s in range(2):
                        gp.wait_ge(b_out[s], 4 * 16)
                    layer_lo(HPAIRS, 0, xn[:, 0, :], 0, False)
                gp.tensor_copy(idx_b[:, 0, :], idx_b0[:, :]).then_inc(idx_next, 1)
                gp.wait_ge(idx_next, BLOCKS * half + 1)
                for n in range(2):
                    if half:
                        gp.wait_ge(up_mm, half * STEPS)
                    gather_b(half, n, n, 0, n)
                step_lo(half, 0, half * STEPS)
                gather_b(half, 2, 2, 0, 0)

            def step_lo(half, slot, n):
                gp.wait_ge(h_hi_done, n + 1)
                gp.tensor_tensor(h_lo[:, slot, :], h[:, :], h_hi[:, slot, :], ALU.subtract
                                 ).then_inc(h_lo_done, 1)

            def body(half, i, last):
                for k in range(BODY):
                    n = half * STEPS + i * BODY + k
                    blk = i * 2 + k // TILES
                    if not (last and k == BODY - 1):
                        step_lo(half, (k + 1) % 2, n + 1)
                    if not (last and k + 3 >= BODY):
                        m = k + 3
                        if m % TILES == 0:
                            next_block(half, (m // TILES) % 2, BLOCKS * half + i * 2 + (m // TILES + 1))
                        wait_before_gather(up_mm, n + 2)
                        gather_b(half, m, m % TILES, (m // TILES) % 2, m % 2)
                    if half == 0:
                        c = k % TILES
                        q = HPAIRS + blk
                        slot = k // TILES
                        if c < 2:
                            gp.wait_ge(layer_add, layer_no(q, c))
                            layer_lo(q, c + 1, xn[:, slot, :], 0, False)
                        elif not (last and slot == 1):
                            if c == 2:
                                if isinstance(q, int):
                                    src = idx_w[:, q + 1, :]
                                else:
                                    src = idx_w[:, bass.ds(q + 1, 1), :].rearrange("p a b -> p (a b)")
                                gp.tensor_copy(idx_now[:, 1 - slot, :], src).then_inc(pool_step, 1)
                                chain_at = chain[0] + i * 2 + (slot + 1)
                                wait_before_gather(pool_step, chain_at)
                                gather_w(None, 1 - slot, 1 - slot)
                            else:
                                layer_lo(q + 1, 0, xn[:, 1 - slot, :], 0, False)

            for half in range(HALVES):
                half_start(half)
                with gp.Fori(0, TURNS - 1) as i:
                    body(half, i, False)
                body(half, TURNS - 1, True)

        @block.scalar
        def _(act):
            def copy(dst, src):
                return act.activation(dst, src, ACT.Copy)

            def bd_high(q, slot, loads):
                act.wait_ge(bd_in[slot], 3 * 16 * loads)
                if isinstance(q, int) and q < HPAIRS:
                    if q >= TP:
                        act.wait_ge(layer_mm, layer_no(q - TP, 2))
                else:
                    act.wait_ge(layer_mm, layer_no(q - 1, 2))
                copy(bd_hi[0:C, :, slot, 0:C], bd_raw[0:C, :, slot, :])
                copy(bd_hi[C:P, :, slot, C:P], bd_raw[C:P, :, slot, :]).then_inc(bd_hi_done, 1)

            def layer_high(q, l, source, slot, first_half):
                hi, _ = layer_in(slot, first_half)
                if first_half:
                    if l:
                        act.wait_ge(layer_add, layer_no(q, l - 1))
                    elif q >= TP:
                        act.wait_ge(layer_mm, layer_no(q - TP, 2))
                copy(hi, source).then_inc(lx_hi, 1)

            def w_high(half, blk, c, slot):
                lo, hi = CHUNKS[c]
                act.wait_ge(raw_in[c], raw_loads(half, blk, c) * 16)
                copy(w_hi[:, slot, lo:hi], w_raw[:, lo:hi]).then_inc(w_hi_done, 1)

            act.sem_inc(silu_done, 1)
            act.wait_ge(consts, 4)
            for j in range(2):
                act.wait_ge(b_in[j], 16)
                copy(u[:, 0, j * BCOLS:(j + 1) * BCOLS], vacc[:, j * BCOLS:(j + 1) * BCOLS]
                     ).then_inc(b_hi_done, 1)
            act.wait_ge(bdn_in, 16)
            copy(bdn_hi[:, :], silu[:, :]).then_inc(bdn_hi_done, 1)

            def start_tile(half, t):
                g = half * TILES + t
                for c in range(KC):
                    act.wait_ge(tr_mm, g * KC + c + 1)
                    copy(xt_hi[:, c, t * TOK:(t + 1) * TOK], (pg + pu)[c][:, :]).then_inc(xt_hi_done, 1)
                for m in range(2):
                    act.wait_ge(a_mm, g * 2 + m + 1)
                    if t:
                        act.wait_ge(sel_mm, g * TP)
                    copy(h_hi[:, m, :], pg[m][:, :]).then_inc(ua_hi, 1)

            for kind, t in start_order():
                if kind == "layers":
                    for j in range(TP):
                        bd_high(t * TP + j, j, t + 1)
                    act.wait_ge(x_in[t], 16)
                    for l in range(LAYERS):
                        for j in range(TP):
                            layer_high(t * TP + j, l, acc[:, t * TP + j, :], j, True)
                    if t == 0:
                        for j in range(2, BCH):
                            act.wait_ge(b_in[j % 2], 32)
                            act.wait_ge(b_out[j % 2], 32)
                            copy(u[:, 0, (j % 2) * BCOLS:(j % 2 + 1) * BCOLS],
                                 vacc[:, (j % 2) * BCOLS:(j % 2 + 1) * BCOLS]).then_inc(b_hi_done, 1)
                        for c in range(ACH):
                            w_high(0, -1, c, 1)
                else:
                    start_tile(0, t)
            bd_high(HPAIRS, 0, TILES + 1)
            act.wait_ge(xn_in[0], 16)
            layer_high(HPAIRS, 0, xn[:, 0, :], 0, False)

            def step_silu(half, n, slot, first=False):
                act.wait_ge(gate_mm, n + 1)
                if not first:
                    act.wait_ge(h_done, hs(n))
                act.activation(silu[:, :], pg[slot][:, :], ACT.Silu).then_inc(silu_done, 1)
                act.wait_ge(h_done, hs(n + 1))
                if not first:
                    act.wait_ge(down_mm, downs((n - 1) * DB))
                copy(h_hi[:, slot, :], h[:, :]).then_inc(h_hi_done, 1)

            def body(half, i, last):
                for k in range(BODY):
                    n = half * STEPS + i * BODY + k
                    blk = i * 2 + k // TILES
                    c = k % TILES
                    if not (last and k == BODY - 1):
                        step_silu(half, n + 1, (k + 1) % 2)
                    if not (last and k // TILES == 1):
                        act.wait_ge(down_mm, downs((n - c) * DB))
                        w_high(half, blk + 1, c, (k // TILES + 1) % 2)
                    if half == 0:
                        q = HPAIRS + blk
                        slot = k // TILES
                        if c < 2:
                            act.wait_ge(layer_add, layer_no(q, c))
                            layer_high(q, c + 1, xn[:, slot, :], 0, False)
                        elif c == 3 and not (last and slot == 1):
                            if slot == 0:
                                bd_high(q + 1, 1, i + (TILES + 1))
                                act.wait_ge(xn_in[1], i * 16 + 16)
                            else:
                                bd_high(q + 1, 0, i + (TILES + 2))
                                act.wait_ge(xn_in[0], i * 16 + 32)
                            layer_high(q + 1, 0, xn[:, 1 - slot, :], 0, False)

            for half in range(HALVES):
                if half:
                    for c in range(ACH):
                        act.wait_ge(down_mm, downs(half * STEPS * DB))
                        w_high(half, -1, c, 1)
                    for t in range(TILES):
                        start_tile(half, t)
                for c in range(NCH):
                    w_high(half, 0, c, 0)
                n0 = half * STEPS
                step_silu(half, n0, 0, first=True)
                with act.Fori(0, TURNS - 1) as i:
                    body(half, i, False)
                body(half, TURNS - 1, True)
                for t in range(TILES):
                    act.wait_ge(v_masked, half * TILES + t + 1)
                    copy(u[:, 0, t * TOK:(t + 1) * TOK], vacc[:, t * TOK:(t + 1) * TOK]
                         ).then_inc(v_hi_done, 1)

        @block.vector
        def _(dve):
            chain = [0]

            def link(ins):
                chain[0] += 1
                ins.then_inc(dve_step, 1)
                dve.wait_ge(dve_step, chain[0])

            dve.sem_inc(h_done, 1)
            dve.sem_inc(down_add, 1)

            dve.wait_ge(consts, 1)
            p0 = p_int[:, 0:1]
            dve.tensor_scalar(p_int[:, 1:2], p0, 4, None, ALU.logical_shift_right)
            dve.tensor_scalar(p_int[:, 2:3], p0, 63, None, ALU.bitwise_and)
            dve.tensor_scalar(p_int[:, 3:4], p0, 5, 1, ALU.logical_shift_right, ALU.bitwise_and)
            dve.tensor_scalar(p_int[:, 4:5], p0, 15, None, ALU.bitwise_and)
            dve.tensor_scalar(r_int2[:, :], r_int[:, :], 15, None, ALU.bitwise_and)
            link(dve.tensor_scalar(p_int[:, 5:6], p0, 6, None, ALU.logical_shift_right))
            dve.tensor_copy(p_f[:, 0:1], p_int[:, 1:2])
            dve.tensor_copy(p_f[:, 1:2], p_int[:, 2:3])
            dve.tensor_copy(half_mask[:, 1:2], p_int[:, 5:6])
            link(dve.tensor_scalar(p_f[:, 2:3], p_int[:, 3:4], float(P), None, ALU.mult))
            link(dve.tensor_tensor(p_f[:, 3:4], p_f[:, 2:3], p_int[:, 4:5], ALU.add))
            link(dve.tensor_scalar(p_f[:, 2:3], p_f[:, 3:4], float(BLOCKS), None, ALU.mult))
            dve.tensor_scalar(half_mask[:, 0:1], half_mask[:, 1:2], -1.0, 1.0, ALU.mult, ALU.add)
            link(dve.memset(pattern[:, :, :], 0.0))
            for part in range(2):
                for term in (part, part + 2):
                    dve.tensor_scalar(pattern[:, part, term * RANK:(term + 1) * RANK], r_int2[:, :],
                                      0.0, None, ALU.is_equal)
            dve.wait_ge(ints_in, 4 * 16)
            for s in range(2):
                rows = slice(s * C, (s + 1) * C)
                by_pair = ints[rows, :, :].rearrange("p k (q s) -> p k q s", s=2)
                dve.tensor_copy(pair_su[rows, :], by_pair[:, 0, :, s])
                dve.tensor_copy(pair_ad[rows, :], by_pair[:, 1, :, s])
            link(dve.tensor_copy(adf[:, :], ints[:, 1, :]))
            dve.tensor_scalar(idx_w[:, :, 0], pair_su[:, :], float(C), p_f[:, 1:2], ALU.mult, ALU.add)
            dve.tensor_scalar(idx_w[:, :, 1], pair_ad[:, :], float(C), p_f[:, 1:2], ALU.mult, ALU.add)
            dve.tensor_scalar(idx_b0[:, :], pair_ad[:, :], float(RANK * BLOCKS), p_f[:, 2:3],
                              ALU.mult, ALU.add).then_inc(idx_done, 1)
            link(dve.tensor_scalar(onehot[:, :], adf[:, :], p_f[:, 0:1], None, ALU.is_equal))
            for a in range(ADAPTERS):
                link(dve.tensor_scalar((bias_n if a else bias)[:, :], pair_ad[:, :], float(a),
                                       bias_src[:, a:a + 1], ALU.is_equal, ALU.mult))
                if a:
                    link(dve.tensor_tensor(bias[:, :], bias[:, :], bias_n[:, :], ALU.add))

            def b_low(j):
                cols = slice((j % 2) * BCOLS, (j % 2 + 1) * BCOLS)
                dve.wait_ge(b_hi_done, j + 1)
                dve.tensor_tensor(u[:, 1, cols], vacc[:, cols], u[:, 0, cols], ALU.subtract
                                  ).then_inc(b_lo_done, 1)

            def bd_low(q, slot):
                dve.wait_ge(bd_hi_done, q + 1)
                dve.tensor_tensor(bd_lo[0:C, :, slot, 0:C], bd_raw[0:C, :, slot, :],
                                  bd_hi[0:C, :, slot, 0:C], ALU.subtract)
                dve.tensor_tensor(bd_lo[C:P, :, slot, C:P], bd_raw[C:P, :, slot, :],
                                  bd_hi[C:P, :, slot, C:P], ALU.subtract).then_inc(bd_lo_done, 1)

            def w_low(half, blk, c, slot):
                lo, hi = CHUNKS[c]
                dve.wait_ge(w_hi_done, conv(half, blk, c))
                dve.tensor_tensor(w_lo[:, slot, lo:hi], w_raw[:, lo:hi], w_hi[:, slot, lo:hi],
                                  ALU.subtract).then_inc(w_done, 1)

            def add_layer(q, l, dst, psum, bias_col):
                dve.wait_ge(layer_mm, layer_no(q, l))
                if l == LAYERS - 1:
                    ins = dve.scalar_tensor_tensor(out=dst, in0=psum[:, :], scalar=bias_col, in1=dst,
                                                   op0=ALU.add, op1=ALU.add)
                else:
                    ins = dve.tensor_tensor(dst, psum[:, :], dst, ALU.add)
                ins.then_inc(layer_add, 1)

            def start_tile(half, t):
                g = half * TILES + t
                for c in range(KC):
                    dve.wait_ge(xt_hi_done, g * KC + c + 1)
                    cols = slice(t * TOK, (t + 1) * TOK)
                    dve.tensor_tensor(xt_lo[:, c, cols], (pg + pu)[c][:, :], xt_hi[:, c, cols],
                                      ALU.subtract).then_inc(xt_done, 1)
                for m in range(2):
                    dve.wait_ge(ua_hi, g * 2 + m + 1)
                    dve.tensor_tensor(h_lo[:, m, :], pg[m][:, :], h_hi[:, m, :], ALU.subtract
                                      ).then_inc(ua_done, 1)
                for j in range(TP):
                    first = 2 * (half * HPAIRS + t * TP + j)
                    if g * TP + j >= 2:
                        dve.wait_ge(sel_mm, g * TP + j - 1)
                    dve.tensor_tensor(
                        sel[:, j % 2],
                        pattern[:, :, :].unsqueeze(2).to_broadcast([P, 2, 2, 4 * RANK]),
                        onehot[:, first:first + 2].unsqueeze(1).unsqueeze(3).to_broadcast([P, 2, 2, 4 * RANK]),
                        ALU.mult).then_inc(sel_done, 1)
                if half == 0 and t == 0:
                    for s in range(2):
                        dve.wait_ge(b_out[s], 4 * 16)
                dve.wait_ge(sel_mm, (g + 1) * TP)
                for m in range(2):
                    dve.tensor_tensor(
                        u[:, m, t * TOK:(t + 1) * TOK].rearrange("p (j s c) -> p j s c", j=TP, s=2),
                        pu[m][:, :].rearrange("p (j s c) -> p j s c", j=TP, s=2),
                        half_mask[:, :].unsqueeze(1).unsqueeze(3).to_broadcast([P, TP, 2, C]),
                        ALU.mult).then_inc(u_done, 1)

            def low_of_layer(q, l, j):
                hi, lo = layer_in(j, True)
                dve.wait_ge(lx_hi, layer_no(q, l))
                dve.tensor_tensor(lo, acc[:, q, :], hi, ALU.subtract).then_inc(lx_lo_v, 1)

            for j in range(2):
                b_low(j)
            dve.wait_ge(bdn_hi_done, 1)
            dve.tensor_tensor(bdn_lo[:, :], silu[:, :], bdn_hi[:, :], ALU.subtract).then_inc(bdn_done, 1)
            for kind, t in start_order():
                if kind == "layers":
                    for j in range(TP):
                        bd_low(t * TP + j, j)
                    for j in (0, 2):
                        low_of_layer(t * TP + j, 0, j)
                    for l in range(LAYERS):
                        for j in range(TP):
                            q = t * TP + j
                            add_layer(q, l, acc[:, q, :], layer_bank[j], bias[:, q:q + 1])
                            if j % 2 == 0 and l + 1 < LAYERS:
                                low_of_layer(q, l + 1, j)
                    if t == 0:
                        for j in range(2, BCH):
                            b_low(j)
                        for c in range(ACH):
                            w_low(0, -1, c, 1)
                else:
                    start_tile(0, t)
            bd_low(HPAIRS, 0)

            def step_h(n, slot):
                dve.wait_ge(up_mm, n + 1)
                dve.wait_ge(silu_done, silus(n + 1))
                dve.tensor_tensor(h[:, :], silu[:, :], pu[slot][:, :], ALU.mult).then_inc(h_done, 1)

            def body(half, i, last):
                for k in range(BODY):
                    n = half * STEPS + i * BODY + k
                    blk = i * 2 + k // TILES
                    t = c = k % TILES
                    if not (last and k == BODY - 1):
                        dve.wait_ge(h_lo_done, n + 1)
                        step_h(n + 1, (k + 1) % 2)
                    for b in range(DB):
                        dve.wait_ge(down_mm, downs(n * DB + (b + 1)))
                        if b == 2:
                            dst, psum = vacc[:, t * TOK:(t + 1) * TOK], pv
                        else:
                            j = b if b < 2 else b - 1
                            dst, psum = acc[:, t * TP + j, :], pd[j % 2]
                        dve.tensor_tensor(dst, psum[:, :], dst, ALU.add).then_inc(down_add, 1)
                    if not (last and k // TILES == 1):
                        w_low(half, blk + 1, c, (k // TILES + 1) % 2)
                    if half == 0:
                        q = HPAIRS + blk
                        slot = k // TILES
                        if c < LAYERS:
                            col = bias[:, bass.ds(q, 1)] if not isinstance(q, int) else bias[:, q:q + 1]
                            add_layer(q, c, xn[:, slot, :], px, col)
                        elif not (last and slot == 1):
                            bd_low(q + 1, 1 - slot)

            for half in range(HALVES):
                if half:
                    for c in range(ACH):
                        w_low(half, -1, c, 1)
                    for t in range(TILES):
                        start_tile(half, t)
                if half:
                    dve.wait_ge(bdown_mm, half * HPAIRS)
                dve.memset(vacc[:, :], 0.0).then_inc(v_zero, 1)
                for c in range(NCH):
                    w_low(half, 0, c, 0)
                dve.wait_ge(v_zero, half + 1)
                step_h(half * STEPS, 0)
                with dve.Fori(0, TURNS - 1) as i:
                    body(half, i, False)
                body(half, TURNS - 1, True)
                for t in range(TILES):
                    cols = slice(t * TOK, (t + 1) * TOK)
                    first = 2 * (half * HPAIRS + t * TP)
                    dve.wait_ge(down_add, adds((half + 1) * STEPS * DB))
                    v3 = vacc[:, cols].rearrange("p (s c) -> p s c", c=C)
                    dve.tensor_tensor(
                        v3, v3, onehot[:, first:first + 2 * TP].unsqueeze(2).to_broadcast([P, 2 * TP, C]),
                        ALU.mult).then_inc(v_masked, 1)
                for t in range(TILES):
                    cols = slice(t * TOK, (t + 1) * TOK)
                    dve.wait_ge(v_hi_done, half * TILES + t + 1)
                    dve.tensor_tensor(u[:, 1, cols], vacc[:, cols], u[:, 0, cols], ALU.subtract
                                      ).then_inc(v_done, 1)
                    for j in range(TP):
                        q = t * TP + j
                        dve.wait_ge(bdown_mm, half * HPAIRS + q + 1)
                        dve.tensor_tensor(acc[:, q, :], pd[q % 2][:, :], acc[:, q, :], ALU.add
                                          ).then_inc(y_add, 1)

        @block.tensor
        def _(pe):
            def split_product(psum, w_parts, x_parts, chunks=1, close=True):
                done = 0
                for c in range(chunks):
                    for wi, xi in ((0, 0), (0, 1), (1, 0)):
                        ins = pe.matmul(psum, w_parts[wi](c), x_parts[xi](c), start=(done == 0),
                                        stop=(close and done == 3 * chunks - 1))
                        done += 1
                return ins

            def layer(q, l, slot, psum, first_half):
                hi, lo = layer_in(slot, first_half)
                if isinstance(q, int) and q < HPAIRS:
                    pe.wait_ge(lx_lo_p if q % 2 else lx_lo_v, lo_no(q, l))
                    if layer_no(q, l) > TP:
                        pe.wait_ge(layer_add, layer_no(q, l) - TP)
                    pe.wait_ge(bd_lo_done, q + 1)
                else:
                    pe.wait_ge(lx_lo_p, lo_no(q, l))
                    pe.wait_ge(layer_add, layer_no(q, l) - 1)
                    pe.wait_ge(bd_lo_done, q + 1)
                split_product(psum[:, :], [lambda c: bd_hi[:, l, slot, :], lambda c: bd_lo[:, l, slot, :]],
                              [lambda c: hi, lambda c: lo]).then_inc(layer_mm, 1)

            def start_tile(half, t):
                g = half * TILES + t
                cols = slice(t * TOK, (t + 1) * TOK)
                if half == 0:
                    pe.wait_ge(layer_add, layer_no(t * TP + TP - 1, LAYERS - 1))
                else:
                    pe.wait_ge(x3_in[t], 16)
                if g:
                    pe.wait_ge(ua_done, g * 2)
                    pe.wait_ge(u_done, g * 2)
                if half and t == 0:
                    pe.wait_ge(h_done, hs(half * STEPS))
                for c in range(KC):
                    for j in range(TP):
                        ins = pe.transpose((pg + pu)[c][:, j * P:(j + 1) * P],
                                           acc[:, t * TP + j, c * P:(c + 1) * P], ident[:, :])
                    ins.then_inc(tr_mm, 1)
                pe.wait_ge(xt_done, (g + 1) * KC)
                pe.wait_ge(w_done, conv(half, -1, ACH - 1))
                for m in range(2):
                    split_product(pg[m][:, :],
                                  [lambda c, w=w: w[:, 1, (m * KC + c) * P:(m * KC + c + 1) * P]
                                   for w in (w_hi, w_lo)],
                                  [lambda c, s=s: s[:, c, cols] for s in (xt_hi, xt_lo)],
                                  chunks=KC).then_inc(a_mm, 1)
                pe.wait_ge(ua_done, (g + 1) * 2)
                for j in range(TP):
                    pe.wait_ge(sel_done, g * TP + j + 1)
                    for m in range(2):
                        for part, src in enumerate((h_hi, h_lo)):
                            ins = pe.matmul(pu[m][:, j * P:(j + 1) * P],
                                            sel[:, j % 2, part].rearrange("p s e -> p (s e)"),
                                            src[:, m, j * P:(j + 1) * P],
                                            start=(part == 0), stop=(part == 1))
                    ins.then_inc(sel_mm, 1)

            def gate_up(half, n, t, wslot, slot, blk, loads, first=False):
                cols = slice(t * TOK, (t + 1) * TOK)
                for m, (psum, base, done, free) in enumerate(((pg[slot], GATE, gate_mm, silu_done),
                                                              (pu[slot], UP, up_mm, h_done))):
                    pe.wait_ge(w_done, conv(half, blk, m))
                    if not first:
                        pe.wait_ge(free, silus(n - 1))
                    split_product(psum[:, :],
                                  [lambda c, w=w: w[:, wslot, base + c * P:base + (c + 1) * P]
                                   for w in (w_hi, w_lo)],
                                  [lambda c, s=s: s[:, c, cols] for s in (xt_hi, xt_lo)],
                                  chunks=KC, close=False)
                    if m == 0:
                        pe.wait_ge(b_got_in[slot], loads)
                    for j in range(TP):
                        ins = pe.matmul(psum[:, j * P:(j + 1) * P], b_got[:, slot, j, m * P:(m + 1) * P],
                                        u[:, m, t * TOK + j * P:t * TOK + (j + 1) * P],
                                        start=False, stop=(j == TP - 1))
                    ins.then_inc(done, 1)

            def down(half, n, wslot, slot, blk, first_of_turn):
                pe.wait_ge(h_lo_done, n + 1)
                pe.wait_ge(w_done, conv(half, blk, NCH - 1))
                for b in range(DB):
                    if b < 2:
                        pe.wait_ge(down_add, adds(n * DB if first_of_turn else n * DB + (b - 1)))
                    elif b > 2:
                        pe.wait_ge(down_add, adds(n * DB + (b - 2)))
                    if b == 2:
                        ins = split_product(pv[:, :],
                                            [lambda c, w=w: w[:, wslot, ADOWN:ADOWN + P] for w in (w_hi, w_lo)],
                                            [lambda c, s=s: s[:, slot, :] for s in (h_hi, h_lo)])
                    else:
                        j = b if b < 2 else b - 1
                        ins = split_product(pd[j % 2][:, :],
                                            [lambda c, s=s: s[:, slot, j * P:(j + 1) * P] for s in (h_hi, h_lo)],
                                            [lambda c, w=w: w[:, wslot, DOWN:DOWN + T] for w in (w_hi, w_lo)])
                    ins.then_inc(down_mm, 1)

            pe.sem_inc(down_mm, 1)
            pe.wait_ge(consts, 4)
            for kind, t in start_order():
                if kind == "layers":
                    for l in range(LAYERS):
                        for j in range(TP):
                            layer(t * TP + j, l, j, layer_bank[j], True)
                else:
                    start_tile(0, t)

            def body(half, i, last):
                for k in range(BODY):
                    n = half * STEPS + i * BODY + k
                    blk = i * 2 + k // TILES
                    if not (last and k == BODY - 1):
                        m = k + 1
                        loads = (half * STEPS + i * BODY + m) * (TP * 8) + (TP * 16 if m % 2 == 0 else TP * 8)
                        gate_up(half, n + 1, m % TILES, (m // TILES) % 2, m % 2, i * 2 + m // TILES, loads)
                    down(half, n, k // TILES, k % 2, blk, k == 0)
                    if half == 0 and k % TILES < LAYERS:
                        layer(HPAIRS + blk, k % TILES, k // TILES, px, False)

            for half in range(HALVES):
                if half:
                    for t in range(TILES):
                        start_tile(half, t)
                g = (half + 1) * TILES
                pe.wait_ge(u_done, g * 2)
                n0 = half * STEPS
                gate_up(half, n0, 0, 0, 0, 0, n0 * TP * 8 + TP * 16, first=True)
                with pe.Fori(0, TURNS - 1) as i:
                    body(half, i, False)
                body(half, TURNS - 1, True)
                pe.wait_ge(bdn_done, 1)
                pe.wait_ge(down_add, adds((half + 1) * STEPS * DB))
                for t in range(TILES):
                    pe.wait_ge(v_done, half * TILES + t + 1)
                    for j in range(TP):
                        q = t * TP + j
                        if q >= 2:
                            pe.wait_ge(y_add, half * HPAIRS + q - 1)
                        split_product(pd[q % 2][:, :],
                                      [lambda c, m=m: u[:, m, q * P:(q + 1) * P] for m in range(2)],
                                      [lambda c, w=w: w[:, :] for w in (bdn_hi, bdn_lo)]
                                      ).then_inc(bdown_mm, 1)


def kernel(x, itok_B_1_198, itok_B_0_7, fside_8xS_0, L0_cond_weights, L1_cond_weights, L2_cond_weights,
           L3_cond_Wg, L3_cond_Wu, L3_cond_Wd, L3_cond_Ag, L3_cond_Bg, L3_cond_Au, L3_cond_Bu,
           L3_cond_Ad, L3_cond_Bd):
    import numpy as np
    import concourse.bacc as bacc
    from concourse.bass_utils import run_bass_kernel_spmd

    def a(v):
        return np.asarray(v)

    def by_block(w):
        return a(w).reshape(KC, P, BLOCKS, P).transpose(2, 1, 0, 3).reshape(BLOCKS, P, KC * P)

    def adapters_in(w):
        return a(w).reshape(ADAPTERS, KC, P, RANK).transpose(2, 1, 0, 3).reshape(P, KC * P)

    def adapters_out(w):
        return a(w).reshape(P, BLOCKS, 1, P)

    arrays = {
        "x": a(x),
        "subject": a(itok_B_1_198),
        "adapter": a(itok_B_0_7),
        "w0_rows": a(L0_cond_weights).reshape(-1, C),
        "w1_rows": a(L1_cond_weights).reshape(-1, C),
        "w2_rows": a(L2_cond_weights).reshape(-1, C),
        "bias_t": a(fside_8xS_0).T,
        "w_all": np.concatenate(
            [by_block(L3_cond_Wg), by_block(L3_cond_Wu), a(L3_cond_Wd).reshape(BLOCKS, P, T),
             a(L3_cond_Ad).reshape(ADAPTERS, BLOCKS, P, RANK).transpose(1, 2, 0, 3).reshape(BLOCKS, P, P)],
            axis=2),
        "a_all": np.concatenate([adapters_in(L3_cond_Ag), adapters_in(L3_cond_Au)], axis=1),
        "b_rows": np.concatenate([adapters_out(L3_cond_Bg), adapters_out(L3_cond_Bu)], axis=2).reshape(P, -1),
        "bd_rows": a(L3_cond_Bd).reshape(P, T),
    }
    arrays = {name: np.ascontiguousarray(v) for name, v in arrays.items()}

    nc = bacc.Bacc("TRN2", target_bir_lowering=False, num_devices=1)
    t = {name: nc.dram_tensor(name, v.shape, mybir.dt.from_np(v.dtype), kind="ExternalInput").ap()
         for name, v in arrays.items()}
    out = nc.dram_tensor("out", (SAMPLES, C, T), F32, kind="ExternalOutput").ap()
    cond_resid_kernel(nc, t["x"], t["subject"], t["adapter"], t["w0_rows"], (t["w1_rows"], t["w2_rows"]),
                      t["bias_t"], t["w_all"], t["a_all"], t["b_rows"], t["bd_rows"], out)
    r = run_bass_kernel_spmd(nc, [arrays], core_ids=[0])
    return r.results[0]["out"]
```

```python
from contextlib import ExitStack

import concourse.bass as bass
from concourse import mybir

F32 = mybir.dt.float32
F32R = mybir.dt.float32r
I32 = mybir.dt.int32
U32 = mybir.dt.uint32
ALU = mybir.AluOpType
ACT = mybir.ActivationFunctionType

P = 128
SAMPLES, C, T = 64, 64, 512
ADAPTERS, RANK = 8, 16
HIDDEN = 2048
KC = T // P
BLOCKS = HIDDEN // P
PAIRS = SAMPLES // 2
HALVES = 2
HPAIRS = PAIRS // HALVES
TP = 4
TILES = HPAIRS // TP
TOK = TP * P
STEPS = BLOCKS * TILES
BODY = 2 * TILES
TURNS = STEPS // BODY

CHUNKS = ((0, 512), (512, 1024), (1024, 1536), (1536, 1664))
WCOLS = CHUNKS[-1][1]
GATE, UP, DOWN, ADOWN = (lo for lo, _ in CHUNKS)
NCH = len(CHUNKS)
ACH = 2
ADAPTERS_IN = -1
FIRST_BLOCK = ((), (), (0, 1), (2, 3))
CONV = ACH + NCH * BLOCKS
DB = TP + 1
BCH = 4
BCOLS = BLOCKS * 2 * P // BCH


def cond_resid_kernel(nc, x, subject, adapter, w0_rows, w1_rows, w2_rows, bias_t, w_all, a_all, b_rows, bd_rows, out):
    b_table = nc.dram_tensor("b_table", (2 * P * BLOCKS, 2 * P), F32).ap()
    e_table = nc.dram_tensor("e_table", (ADAPTERS * C, C), F32).ap()
    x3_next = nc.dram_tensor("x3_next", (HPAIRS, P, T), F32).ap()

    with ExitStack() as ctx:
        def sb(name, shape, dt=F32):
            return ctx.enter_context(nc.sbuf_tensor(name, shape, dt))

        def bank(name):
            return ctx.enter_context(nc.psum_tensor(name, [P, 512], F32))

        def sem(name):
            return ctx.enter_context(nc.semaphore(name))

        xt_hi = sb("xt_hi", [P, KC, TILES * TOK], F32R)
        xt_lo = sb("xt_lo", [P, KC, TILES * TOK], F32R)
        acc = sb("acc", [P, HPAIRS, T])
        u = sb("u", [P, 2, TILES * TOK], F32R)
        vacc = sb("vacc", [P, TILES * TOK])
        w_raw = sb("w_raw", [P, WCOLS])
        w_hi = sb("w_hi", [P, 2, WCOLS], F32R)
        w_lo = sb("w_lo", [P, 2, WCOLS], F32R)
        b_got = sb("b_got", [P, 2, TP, 2 * P], F32R)
        silu = sb("silu", [P, TOK])
        h = sb("h", [P, TOK])
        h_hi = sb("h_hi", [P, 2, TOK], F32R)
        h_lo = sb("h_lo", [P, 2, TOK], F32R)
        xn = sb("xn", [P, 2, T])
        xn_hi = sb("xn_hi", [P, T], F32R)
        xn_lo = sb("xn_lo", [P, T], F32R)
        ya_hi = sb("ya_hi", [P, T], F32R)
        ya_lo = sb("ya_lo", [P, T], F32R)
        et_hi = sb("et_hi", [P, TP, P], F32R)
        et_lo = sb("et_lo", [P, TP, P], F32R)
        eb_hi = sb("eb_hi", [P, TP, C], F32R)
        eb_lo = sb("eb_lo", [P, TP, C], F32R)
        eb_raw = sb("eb_raw", [P, TP, C])
        e_sum = sb("e_sum", [P, TP, C])
        ea_one = sb("ea_one", [P, 1, P])
        em_one = sb("em_one", [P, 1, P])
        bd_hi = sb("bd_hi", [P, TP, P], F32R)
        bd_lo = sb("bd_lo", [P, TP, P], F32R)
        bdn_hi = sb("bdn_hi", [P, T], F32R)
        bdn_lo = sb("bdn_lo", [P, T], F32R)
        ident = sb("ident", [P, P])
        pattern = sb("pattern", [P, 2, 4 * RANK])
        sel = sb("sel", [P, 2, 2, 2, 4 * RANK], F32R)
        ints = sb("ints", [P, 2, SAMPLES], I32)
        adf = sb("adf", [P, SAMPLES])
        pair_ad = sb("pair_ad", [P, PAIRS])
        pair_su = sb("pair_su", [P, PAIRS])
        onehot = sb("onehot", [P, SAMPLES])
        bias = sb("bias", [P, PAIRS])
        bias_n = sb("bias_n", [P, PAIRS])
        bias_src = sb("bias_src", [P, ADAPTERS])
        p_int = sb("p_int", [P, 8], I32)
        p_f = sb("p_f", [P, 4])
        half_mask = sb("half_mask", [P, 2])
        r_int = sb("r_int", [P, RANK], I32)
        r_int2 = sb("r_int2", [P, RANK], I32)
        idx_w = sb("idx_w", [P, PAIRS, 2], I32)
        idx_b0 = sb("idx_b0", [P, PAIRS], I32)
        idx_b = sb("idx_b", [P, 2, PAIRS], I32)
        idx_now = sb("idx_now", [P, 2], I32)

        pg = [bank(f"pg{i}") for i in range(2)]
        pu = [bank(f"pu{i}") for i in range(2)]
        pd = [bank(f"pd{i}") for i in range(2)]
        pv = bank("pv")
        px = bank("px")
        layer_bank = [pv, pd[0], pd[1], px]

        def four(ap):
            return ap.rearrange("p (j n) -> p j n", j=TP)

        ea_four = [four(a) for a in (xn[:, 0, :], acc[:, 12, :], acc[:, 13, :], acc[:, 14, :], xn[:, 0, :])]
        eb_four = [eb_raw[:, :, :], four(acc[:, 15, 0:TP * C]), four(acc[:, 15, TP * C:2 * TP * C]),
                   four(h[:, 0:TP * C]), eb_raw[:, :, :]]
        em_four = four(xn[:, 1, :])
        b_raws = [vacc[:, 0:BCOLS], vacc[:, BCOLS:2 * BCOLS],
                  acc[:, 8:10, :].rearrange("p j n -> p (j n)"), acc[:, 10:12, :].rearrange("p j n -> p (j n)")]
        b_parts = [[u[:, part, j * BCOLS:(j + 1) * BCOLS] for part in range(2)] for j in range(2)] \
            + [[xt[:, j, TOK:TOK + BCOLS] for xt in (xt_hi, xt_lo)] for j in range(2)]

        ints_in = sem("ints_in")
        e0_in = sem("e0_in")
        x_in = [sem(f"x_in{t}") for t in range(TILES)]
        b_in = [sem(f"b_in{i}") for i in range(BCH)]
        bdn_in = sem("bdn_in")
        raw_in = [sem(f"raw_in{c}") for c in range(NCH)]
        b_out = [sem(f"b_out{i}") for i in range(2)]
        e_out = sem("e_out")
        x3_out = [sem(f"x3_out{i}") for i in range(2)]
        x3_in = [sem(f"x3_in{t}") for t in range(TILES)]
        xn_in = [sem(f"xn_in{i}") for i in range(2)]
        y_out = [sem(f"y_out{t}") for t in range(TILES)]
        e_in = sem("e_in")
        e_tile_in = [sem(f"e_tile_in{t}") for t in range(TILES)]
        b_got_in = [sem(f"b_got_in{i}") for i in range(2)]
        consts = sem("consts")
        pool_step = sem("pool_step")
        dve_step = sem("dve_step")
        mask_done = sem("mask_done")
        idx_done = sem("idx_done")
        b_hi_done = sem("b_hi_done")
        b_lo_done = sem("b_lo_done")
        bdn_done = sem("bdn_done")
        bdn_hi_done = sem("bdn_hi_done")
        e_t_done = sem("e_t_done")
        e_hi_done = sem("e_hi_done")
        e_lo_done = sem("e_lo_done")
        e_sum_done = sem("e_sum_done")
        e_mm = sem("e_mm")
        e_add = sem("e_add")
        e_masked = sem("e_masked")
        bd_hi_done = sem("bd_hi_done")
        bd_done = sem("bd_done")
        lx_hi = sem("lx_hi")
        lx_lo_p = sem("lx_lo_p")
        lx_lo_v = sem("lx_lo_v")
        layer_mm = sem("layer_mm")
        layer_add = sem("layer_add")
        tr_mm = sem("tr_mm")
        xt_hi_done = sem("xt_hi_done")
        xt_done = sem("xt_done")
        a_mm = sem("a_mm")
        ua_hi = sem("ua_hi")
        ua_done = sem("ua_done")
        sel_done = sem("sel_done")
        sel_mm = sem("sel_mm")
        u_done = sem("u_done")
        v_zero = sem("v_zero")
        w_hi_done = sem("w_hi_done")
        w_done = sem("w_done")
        gate_mm = sem("gate_mm")
        up_mm = sem("up_mm")
        silu_done = sem("silu_done")
        h_done = sem("h_done")
        h_hi_done = sem("h_hi_done")
        h_lo_done = sem("h_lo_done")
        down_mm = sem("down_mm")
        down_add = sem("down_add")
        v_masked = sem("v_masked")
        v_hi_done = sem("v_hi_done")
        v_done = sem("v_done")
        bdown_mm = sem("bdown_mm")
        y_add = sem("y_add")
        idx_next = sem("idx_next")
        may_gather = sem("may_gather")

        block = ctx.enter_context(nc.Block())

        def conv(half, blk, c):
            if isinstance(blk, int) and blk == ADAPTERS_IN:
                return CONV * half + NCH + c + 1
            if isinstance(blk, int) and blk == 0:
                return CONV * half + c + 1
            return blk * NCH + (CONV * half + ACH + c + 1)

        def raw_loads(half, blk, c):
            if c >= ACH:
                return blk + (BLOCKS * half + 1)
            if isinstance(blk, int) and blk <= 0:
                return (BLOCKS + 1) * half + (2 if blk == ADAPTERS_IN else 1)
            return blk + ((BLOCKS + 1) * half + 2)

        def silus(n): return n + 1
        def hs(n): return n + 1
        def downs(n): return n + 1
        def adds(n): return n + 1

        def comb(q):
            return q + (TILES + 1 - HPAIRS)

        def layer_in(j, first_half):
            if first_half:
                tail = slice((TILES - 1) * TOK, TILES * TOK)
                return xt_hi[:, j, tail], xt_lo[:, j, tail]
            return xn_hi[:, :], xn_lo[:, :]

        def lows(q):
            if isinstance(q, int) and q < HPAIRS:
                return q // 2 + 1
            return q + (HPAIRS // 2 - HPAIRS + 1)

        ua_parts = [(xn_hi[:, :], xn_lo[:, :]), (ya_hi[:, :], ya_lo[:, :])]

        def tile_banks(t):
            if t == 0:
                return pg + pu, pg, pu
            return [pd[0], pd[1], pv, px], pd, [px, pv]

        OPENING = (("comb_in", 0), ("comb_out", 0), ("b", 0), ("b", 1), ("b", 2), ("b", 3), ("x", 0),
                   ("comb_in", 1), ("comb_out", 1), ("layer", 0), ("x", 1), ("comb_in", 2), ("comb_out", 2), ("w", 0),
                   ("transpose", 0), ("w", ADAPTERS_IN), ("layer", 1), ("x", 2), ("products", 0),
                   ("comb_in", 3), ("comb_out", 3), ("select", 0))
        AFTER_FIRST = (("layer", 2), ("x", 3), ("comb_in", 4), ("comb_out", 4))

        @block.sync
        def _(sp):
            def load_raw(half, blk, c):
                lo, hi = CHUNKS[c]
                if not isinstance(blk, int):
                    src = w_all[bass.ds(blk, 1), :, lo:hi].rearrange("a p n -> (a p) n")
                elif blk == ADAPTERS_IN:
                    src = a_all[:, lo:hi]
                else:
                    src = w_all[blk, :, lo:hi]
                sp.dma_start(w_raw[:, lo:hi], src).then_inc(raw_in[c], 16)

            def load_x(t):
                src = x[2 * TP * t:2 * TP * (t + 1)].rearrange("(q s) c t -> (s c) q t", s=2)
                sp.dma_start(acc[:, TP * t:TP * (t + 1), :], src).then_inc(x_in[t], 16)

            def load_b(j):
                sp.dma_start(b_raws[j], b_rows[:, j * BCOLS:(j + 1) * BCOLS]).then_inc(b_in[j], 16)

            def store_b(j):
                sp.wait_ge(b_lo_done, j + 1)
                table = b_table.rearrange("(g p k) n -> g p (k n)", g=2, k=BLOCKS)
                for part in range(2):
                    sp.dma_start(table[part, :, j * BCOLS:(j + 1) * BCOLS],
                                 b_parts[j][part].bitcast(F32)).then_inc(b_out[j % 2], 16)

            def load_xn(q, slot):
                src = (x[2 * q:2 * q + 2] if isinstance(q, int) else x[bass.ds(q * 2, 2)])
                sp.dma_start(xn[:, slot, :], src.rearrange("s c t -> (s c) t")).then_inc(xn_in[slot], 16)

            sp.dma_start(ea_four[0], w1_rows.rearrange("(j p) n -> p j n", p=P)).then_inc(e0_in, 16)
            sp.dma_start(eb_four[0], w2_rows.rearrange("(j p) n -> p j n", p=P)).then_inc(e0_in, 16)
            sp.dma_start(ints[:, 0, :], subject.partition_broadcast(P)).then_inc(ints_in, 16)
            sp.dma_start(ints[:, 1, :], adapter.partition_broadcast(P)).then_inc(ints_in, 16)
            for s in range(2):
                sp.dma_start(bias_src[s * C:(s + 1) * C, :], bias_t).then_inc(ints_in, 16)
            load_b(0)
            load_b(1)
            load_x(0)
            load_b(2)
            load_b(3)
            sp.wait_ge(e_add, 1)
            sp.dma_start(e_table.rearrange("(j p) n -> p j n", p=P), e_sum[:, :, :]).then_inc(e_out, 16)
            load_x(1)
            sp.wait_ge(e_tile_in[0], 2 * TP * 16)
            for j in range(BCH):
                store_b(j)
            for c in range(NCH):
                load_raw(0, 0, c)
            sp.wait_ge(e_tile_in[1], 2 * TP * 16)
            load_x(2)
            sp.dma_start(silu[:, :], bd_rows).then_inc(bdn_in, 16)
            for c in range(ACH):
                sp.wait_ge(w_done, conv(0, 0, c))
                load_raw(0, ADAPTERS_IN, c)
            for c in range(ACH, NCH):
                sp.wait_ge(w_done, conv(0, 0, c))
                load_raw(0, 1, c)
            sp.wait_ge(e_sum_done, TILES)
            load_x(3)
            sp.wait_ge(bd_done, TILES)
            load_xn(HPAIRS, 0)
            load_xn(HPAIRS + 1, 1)

            def store_y(half, t):
                first = 2 * TP * (half * TILES + t)
                sp.wait_ge(y_add, half * HPAIRS + TP * (t + 1))
                sp.dma_start(out[first:first + 2 * TP].rearrange("(q s) c t -> (s c) q t", s=2),
                             acc[:, TP * t:TP * (t + 1), :]).then_inc(y_out[t], 16)

            def load_x3(t):
                sp.wait_ge(y_out[t], 16)
                sp.dma_start(acc[:, TP * t:TP * (t + 1), :],
                             x3_next[TP * t:TP * (t + 1)].rearrange("q p t -> p q t")).then_inc(x3_in[t], 16)

            def after_conversion(half, i, k, last):
                blk = i * 2 + k // TILES
                if isinstance(i, int) and i == 0 and k < TILES:
                    chunks = FIRST_BLOCK[k]
                else:
                    chunks = (k % TILES,)
                for c in chunks:
                    if not last:
                        sp.wait_ge(w_done, conv(half, blk + 1, c))
                        load_raw(half, blk + 2, c)
                    elif half + 1 < HALVES:
                        if k < TILES:
                            sp.wait_ge(w_done, conv(half, blk + 1, c))
                            load_raw(half + 1, 0, c)
                        else:
                            sp.wait_ge(w_done, conv(half + 1, 0, c))
                            load_raw(half + 1, ADAPTERS_IN if c < ACH else 1, c)

            def body(half, i, last):
                for k in range(BODY):
                    blk = i * 2 + (k // TILES)
                    after_conversion(half, i, k, last)
                    if last and k >= TILES + 1:
                        store_y(half, k - TILES - 1)
                    if last and half == 0 and k >= TILES + 2:
                        if k == BODY - 1:
                            sp.wait_ge(x3_out[0], TURNS * 16)
                            sp.wait_ge(x3_out[1], TURNS * 16 - 16)
                        else:
                            sp.wait_ge(x3_out[0], TURNS * 16 - 16)
                            sp.wait_ge(x3_out[1], TURNS * 16 - 16)
                        load_x3(k - TILES - 2)
                    if half == 0 and k % TILES == TILES - 1:
                        slot = k // TILES
                        q = blk + HPAIRS
                        sp.wait_ge(layer_add, q + 1)
                        if isinstance(blk, int):
                            dst = x3_next[blk]
                        else:
                            dst = x3_next[bass.ds(blk, 1)].rearrange("a p t -> (a p) t")
                        sp.dma_start(dst, xn[:, slot, :]).then_inc(x3_out[slot], 16)
                        if not last:
                            sp.wait_ge(x3_out[slot], i * 16 + 16)
                            load_xn(q + 2, slot)

            for half in range(HALVES):
                for c in range(ACH):
                    sp.wait_ge(w_done, conv(half, ADAPTERS_IN, c))
                    load_raw(half, 1, c)
                body(half, 0, False)
                with sp.Fori(1, TURNS - 1) as i:
                    body(half, i, False)
                body(half, TURNS - 1, True)
                if half == 0:
                    load_x3(TILES - 2)
                store_y(half, TILES - 1)
                if half == 0:
                    sp.wait_ge(x3_out[1], TURNS * 16)
                    load_x3(TILES - 1)
            for t in range(TILES):
                sp.wait_ge(y_out[t], 2 * 16)
            for s in range(2):
                sp.wait_ge(b_out[s], 4 * 16)
            sp.wait_ge(e_out, 16)

        @block.gpsimd
        def _(gp):
            chain = [0]

            def link(ins):
                chain[0] += 1
                ins.then_inc(pool_step, 1)
                gp.wait_ge(pool_step, chain[0])

            gp.iota(p_int[:, 0:1], [[0, 1]], base=0, channel_multiplier=1).then_inc(consts, 1)
            gp.iota(r_int[:, :], [[1, RANK]], base=P, channel_multiplier=-1).then_inc(consts, 1)
            link(gp.memset(ident[:, :], 0.0))
            gp.affine_select(out=ident[:, :], in_=ident[:, :], compare_op=ALU.not_equal, fill=1.0, base=0,
                             pattern=[[-1, P]], channel_multiplier=1).then_inc(consts, 1)

            def wait_before_gather(semaphore, value):
                gp.wait_ge(semaphore, value)
                gp.sem_inc(may_gather, 1)

            def gather_rows(dst, table, rows, semaphore):
                gp.indirect_dma_start(out=dst, out_offset=None, in_=table,
                                      in_offset=bass.IndirectOffsetOnAxis(ap=rows.bitcast(U32), axis=0)
                                      ).then_inc(semaphore, 16)

            def gather_tile(e):
                gp.wait_ge(idx_done, 1)
                gp.wait_ge(e_sum_done, 1)
                for j in range(TP):
                    q = (e - 1) * TP + j
                    gather_rows(ea_four[e][:, j, :], w0_rows, idx_w[:, q, 0:1], e_tile_in[e - 1])
                gp.wait_ge(e_out, 16)
                for j in range(TP):
                    q = (e - 1) * TP + j
                    gather_rows(eb_four[e][:, j, :], e_table, idx_w[:, q, 1:2], e_tile_in[e - 1])

            def gather_b(half, m, parity, slot):
                for j in range(TP):
                    q = half * HPAIRS + (m % TILES) * TP + j
                    gp.indirect_dma_start(
                        out=b_got[:, slot, j, :].bitcast(F32), out_offset=None, in_=b_table,
                        in_offset=bass.IndirectOffsetOnAxis(ap=idx_b[:, parity, q:q + 1].bitcast(U32), axis=0)
                    ).then_inc(b_got_in[slot], 16)

            def comb_in(e):
                gp.wait_ge(e_hi_done, e + 1)
                gp.tensor_tensor(et_lo[:, 0:1, :], em_one[:, :, :], et_hi[:, 0:1, :], ALU.subtract)
                gp.tensor_tensor(eb_lo[:, 0:1, :], eb_raw[:, 0:1, :], eb_hi[:, 0:1, :], ALU.subtract
                                 ).then_inc(e_lo_done, 1)
                gp.wait_ge(e_masked, e - 1)
                gp.tensor_tensor(e_sum[:, 0:1, :], ea_one[:, :, 0:C], eb_raw[:, 0:1, :], ALU.add
                                 ).then_inc(e_sum_done, 1)

            def comb_out(e):
                gp.wait_ge(bd_hi_done, e)
                gp.tensor_tensor(bd_lo[:, 0:1, :], em_one[:, :, :], bd_hi[:, 0:1, :], ALU.subtract
                                 ).then_inc(bd_done, 1)

            def split_x(q, j, source, first_half):
                hi, lo = layer_in(j, first_half)
                gp.wait_ge(lx_hi, q + 1)
                gp.tensor_tensor(lo, source, hi, ALU.subtract).then_inc(lx_lo_p, 1)

            def next_block(parity, count):
                gp.tensor_scalar(idx_b[:, parity, :], idx_b[:, 1 - parity, :], 1.0, None, ALU.add
                                 ).then_inc(idx_next, 1)
                wait_before_gather(idx_next, count)

            def split_odd(t):
                for j in (1, 3):
                    split_x(t * TP + j, j, acc[:, t * TP + j, :], True)

            def step_lo(slot, n):
                gp.wait_ge(h_hi_done, n + 1)
                gp.tensor_tensor(h_lo[:, slot, :], h[:, :], h_hi[:, slot, :], ALU.subtract
                                 ).then_inc(h_lo_done, 1)

            def half_start(half):
                if half == 0:
                    for s in range(2):
                        gp.wait_ge(b_out[s], 4 * 16)
                gp.tensor_copy(idx_b[:, 0, :], idx_b0[:, :]).then_inc(idx_next, 1)
                gp.wait_ge(idx_next, BLOCKS * half + 1)
                if half:
                    gp.wait_ge(up_mm, half * STEPS)
                for m in range(2):
                    gather_b(half, m, 0, m)
                if half:
                    clear_v(TILES - 1)
                else:
                    gather_tile(3)
                    split_odd(2)
                step_lo(0, half * STEPS)
                gather_b(half, 2, 0, 0)
                if half == 0:
                    gather_tile(4)
                    split_odd(3)

            def clear_v(t):
                gp.wait_ge(v_done, t + 1)
                gp.memset(vacc[:, t * TOK:(t + 1) * TOK], 0.0).then_inc(v_zero, 1)

            def body(half, i, last):
                for k in range(BODY):
                    n = i * BODY + (half * STEPS + k)
                    c, slot = k % TILES, k // TILES
                    if not (last and k == BODY - 1):
                        step_lo((k + 1) % 2, n + 1)
                    if not (last and k + 3 >= BODY):
                        m = k + 3
                        if m % TILES == 0:
                            next_block((m // TILES) % 2, i * 2 + (BLOCKS * half + m // TILES + 1))
                        wait_before_gather(up_mm, n + 2)
                        gather_b(half, m, (m // TILES) % 2, m % 2)
                    if half == 0:
                        q = i * 2 + (HPAIRS + slot)
                        e = comb(q)
                        if c == 0:
                            src = (idx_w[:, q, :] if isinstance(q, int)
                                   else idx_w[:, bass.ds(q, 1), :].rearrange("p a b -> p (a b)"))
                            gp.tensor_copy(idx_now[:, :], src).then_inc(pool_step, 1)
                            gp.wait_ge(e_sum_done, e)
                            wait_before_gather(pool_step, i * 2 + (chain[0] + slot + 1))
                            gather_rows(ea_one[:, 0, :], w0_rows, idx_now[:, 0:1], e_in)
                            gather_rows(eb_raw[:, 0, :], e_table, idx_now[:, 1:2], e_in)
                        elif c == 1:
                            comb_in(e)
                        elif c == 2:
                            split_x(q, 0, xn[:, slot, :], False)
                            comb_out(e)
                        if last and k > TILES:
                            clear_v(k - TILES - 1)

            for t in range(2):
                gather_tile(t + 1)
                split_odd(t)
            for half in range(HALVES):
                half_start(half)
                body(half, 0, False)
                with gp.Fori(1, TURNS - 1) as i:
                    body(half, i, False)
                body(half, TURNS - 1, True)

        @block.scalar
        def _(act):
            def copy(dst, src):
                return act.activation(dst, src, ACT.Copy)

            def comb_in(e, n):
                act.wait_ge(e_t_done, e + 1)
                if not (isinstance(e, int) and e == 0):
                    act.wait_ge(e_mm, e)
                copy(et_hi[:, 0:n, :], (em_four if n == TP else em_one)[:, 0:n, :])
                copy(eb_hi[:, 0:n, :], eb_four[e] if n == TP else eb_raw[:, 0:n, :]).then_inc(e_hi_done, 1)

            def comb_out(e, n, layers):
                act.wait_ge(e_masked, e)
                if not (isinstance(layers, int) and layers == 0):
                    act.wait_ge(layer_mm, layers)
                em = em_four if n == TP else em_one
                copy(bd_hi[:, 0:n, :], em[:, 0:n, :]).then_inc(bd_hi_done, 1)

            def split_x(q, j, source, first_half):
                hi, _ = layer_in(j, first_half)
                copy(hi, source).then_inc(lx_hi, 1)

            def w_high(half, blk, c, slot):
                lo, hi = CHUNKS[c]
                act.wait_ge(raw_in[c], raw_loads(half, blk, c) * 16)
                copy(w_hi[:, slot, lo:hi], w_raw[:, lo:hi]).then_inc(w_hi_done, 1)

            def transpose(half, t):
                g = half * TILES + t
                if g == 1:
                    for s in range(2):
                        act.wait_ge(b_out[s], 4 * 16)
                for c, psum in enumerate(tile_banks(t)[0]):
                    act.wait_ge(tr_mm, g * KC + c + 1)
                    copy(xt_hi[:, c, t * TOK:(t + 1) * TOK], psum[:, :]).then_inc(xt_hi_done, 1)

            def products(half, t):
                g = half * TILES + t
                for m, psum in enumerate(tile_banks(t)[1]):
                    act.wait_ge(a_mm, g * 2 + m + 1)
                    if g:
                        act.wait_ge(sel_mm, g * TP)
                    if half:
                        act.wait_ge(layer_mm, PAIRS)
                    copy(ua_parts[m][0], psum[:, :]).then_inc(ua_hi, 1)

            def opening(events):
                for what, m in events:
                    if what == "comb_in":
                        comb_in(m, TP)
                    elif what == "comb_out" and m:
                        comb_out(m, TP, (m - 1) * TP)
                    elif what == "b":
                        act.wait_ge(b_in[m], 16)
                        copy(b_parts[m][0], b_raws[m]).then_inc(b_hi_done, 1)
                    elif what == "x":
                        act.wait_ge(x_in[m], 16)
                        if m:
                            act.wait_ge(layer_mm, m * TP)
                        for j in range(TP):
                            split_x(m * TP + j, j, acc[:, m * TP + j, :], True)
                    elif what == "w":
                        for c in range(ACH if m == ADAPTERS_IN else NCH):
                            w_high(0, m, c, 1 if m == ADAPTERS_IN else 0)
                    elif what == "transpose":
                        transpose(0, m)
                    elif what == "products":
                        products(0, m)

            def step_silu(n, slot):
                act.wait_ge(gate_mm, n + 1)
                act.wait_ge(h_done, hs(n))
                act.activation(silu[:, :], pg[slot][:, :], ACT.Silu).then_inc(silu_done, 1)

            def step_hi(n, slot, first=False):
                act.wait_ge(h_done, hs(n + 1))
                if not first:
                    act.wait_ge(down_mm, downs((n - 1) * DB))
                copy(h_hi[:, slot, :], h[:, :]).then_inc(h_hi_done, 1)

            def v_high(half, t):
                cols = slice(t * TOK, (t + 1) * TOK)
                act.wait_ge(v_masked, half * TILES + t + 1)
                act.wait_ge(up_mm, (half + 1) * STEPS - TILES + t + 1)
                copy(u[:, 0, cols], vacc[:, cols]).then_inc(v_hi_done, 1)

            def body(half, i, last):
                first = isinstance(i, int) and i == 0
                for k in range(BODY):
                    n = i * BODY + (half * STEPS + k)
                    c, slot = k % TILES, k // TILES
                    blk = i * 2 + slot
                    if last and k > TILES:
                        v_high(half, k - TILES - 1)
                    if first and k + 2 < TILES:
                        transpose(half, k + 2)
                    if not (last and k == BODY - 1):
                        step_silu(n + 1, (k + 1) % 2)
                    if first and k + 2 < TILES:
                        products(half, k + 2)
                    if not (last and k == BODY - 1):
                        step_hi(n + 1, (k + 1) % 2)
                    if first and slot == 0:
                        for ch in FIRST_BLOCK[k]:
                            if half == 0 and ch == 0:
                                act.wait_ge(a_mm, 2 * TILES)
                            elif half:
                                act.wait_ge(a_mm, 2 * TILES * HALVES)
                            w_high(half, 1, ch, 1)
                    elif not (last and (slot == 1 and half + 1 == HALVES)):
                        act.wait_ge(down_mm, downs((n - c) * DB))
                        if last and slot == 1:
                            w_high(half + 1, 0, c, 0)
                        else:
                            w_high(half, blk + 1, c, 1 - slot)
                    if half == 0:
                        q = i * 2 + (HPAIRS + slot)
                        e = comb(q)
                        if c == 1:
                            comb_in(e, 1)
                        elif c == 2:
                            if first and slot == 0:
                                act.wait_ge(sel_mm, TILES * TP)
                            act.wait_ge(layer_mm, q)
                            act.wait_ge(xn_in[slot], i * 16 + 16)
                            split_x(q, 0, xn[:, slot, :], False)
                            comb_out(e, 1, q)

            opening(OPENING)
            act.wait_ge(bdn_in, 16)
            copy(bdn_hi[:, :], silu[:, :]).then_inc(bdn_hi_done, 1)
            act.wait_ge(bdn_done, 1)
            act.sem_inc(silu_done, 1)
            for half in range(HALVES):
                if half:
                    for c in range(ACH):
                        act.wait_ge(up_mm, half * STEPS)
                        w_high(half, ADAPTERS_IN, c, 1)
                    transpose(half, 0)
                    v_high(half - 1, TILES - 1)
                    products(half, 0)
                transpose(half, 1)
                step_silu(half * STEPS, 0)
                products(half, 1)
                step_hi(half * STEPS, 0, first=True)
                if half == 0:
                    opening(AFTER_FIRST)
                body(half, 0, False)
                with act.Fori(1, TURNS - 1) as i:
                    body(half, i, False)
                body(half, TURNS - 1, True)
            v_high(HALVES - 1, TILES - 1)

        @block.vector
        def _(dve):
            chain = [0]

            def link(ins):
                chain[0] += 1
                ins.then_inc(dve_step, 1)
                dve.wait_ge(dve_step, chain[0])

            def masked(dst, src, n):
                return dve.tensor_tensor(
                    dst[:, 0:n, :].rearrange("p j (s d) -> p j s d", s=2),
                    src.unsqueeze(2).to_broadcast([P, n, 2, C]),
                    half_mask[:, :].unsqueeze(1).unsqueeze(3).to_broadcast([P, n, 2, C]), ALU.mult)

            def comb_in(e):
                if e == 0:
                    dve.wait_ge(e0_in, 2 * 16)
                else:
                    dve.wait_ge(e_tile_in[e - 1], 2 * TP * 16)
                if e >= 2:
                    dve.wait_ge(bd_done, e - 1)
                elif e == 1:
                    dve.wait_ge(e_lo_done, 1)
                masked(em_four, ea_four[e][:, :, C:2 * C], TP).then_inc(e_t_done, 1)
                if e == 0:
                    numbers()
                if e == 1:
                    dve.wait_ge(e_out, 16)
                elif e >= 2:
                    dve.wait_ge(e_masked, e - 1)
                dve.tensor_tensor(e_sum[:, :, :], ea_four[e][:, :, 0:C], eb_four[e], ALU.add
                                  ).then_inc(e_sum_done, 1)
                dve.wait_ge(e_hi_done, e + 1)
                dve.tensor_tensor(et_lo[:, :, :], em_four, et_hi[:, :, :], ALU.subtract)
                dve.tensor_tensor(eb_lo[:, :, :], eb_four[e], eb_hi[:, :, :], ALU.subtract
                                  ).then_inc(e_lo_done, 1)

            def comb_in_one(e):
                dve.wait_ge(e_in, (e - TILES) * 2 * 16)
                dve.wait_ge(bd_done, e - 1)
                masked(em_one, ea_one[:, :, C:2 * C], 1).then_inc(e_t_done, 1)

            def comb_out(e, n):
                dve.wait_ge(e_mm, e + 1)
                dve.wait_ge(e_sum_done, e + 1)
                dve.tensor_tensor(e_sum[:, 0:n, :], px[:, 0:n * C].rearrange("p (j d) -> p j d", j=n),
                                  e_sum[:, 0:n, :], ALU.add).then_inc(e_add, 1)
                if not (isinstance(e, int) and e == 0):
                    dve.wait_ge(e_add, e + 1)
                    masked(em_four if n == TP else em_one, e_sum[:, 0:n, :], n).then_inc(e_masked, 1)
                if isinstance(e, int) and 0 < e <= TILES:
                    dve.wait_ge(bd_hi_done, e)
                    dve.tensor_tensor(bd_lo[:, :, :], em_four, bd_hi[:, :, :], ALU.subtract
                                      ).then_inc(bd_done, 1)

            def w_low(half, blk, c, slot):
                lo, hi = CHUNKS[c]
                dve.wait_ge(w_hi_done, conv(half, blk, c))
                dve.tensor_tensor(w_lo[:, slot, lo:hi], w_raw[:, lo:hi], w_hi[:, slot, lo:hi],
                                  ALU.subtract).then_inc(w_done, 1)

            def add_layer(q, dst, psum, bias_col):
                dve.wait_ge(layer_mm, q + 1)
                dve.scalar_tensor_tensor(out=dst, in0=psum[:, :], scalar=bias_col, in1=dst,
                                         op0=ALU.add, op1=ALU.add).then_inc(layer_add, 1)

            def transpose(half, t):
                g = half * TILES + t
                cols = slice(t * TOK, (t + 1) * TOK)
                for c, psum in enumerate(tile_banks(t)[0]):
                    dve.wait_ge(xt_hi_done, g * KC + c + 1)
                    dve.tensor_tensor(xt_lo[:, c, cols], psum[:, :], xt_hi[:, c, cols], ALU.subtract
                                      ).then_inc(xt_done, 1)

            def products(half, t):
                g = half * TILES + t
                for m, psum in enumerate(tile_banks(t)[1]):
                    dve.wait_ge(ua_hi, g * 2 + m + 1)
                    dve.tensor_tensor(ua_parts[m][1], psum[:, :], ua_parts[m][0], ALU.subtract
                                      ).then_inc(ua_done, 1)
                selectors(half, t, (0, 1))

            def selectors(half, t, pairs):
                g = half * TILES + t
                for j in pairs:
                    first = 2 * (half * HPAIRS + t * TP + j)
                    if g * TP + j >= 2:
                        dve.wait_ge(sel_mm, g * TP + j - 1)
                    dve.tensor_tensor(
                        sel[:, j % 2],
                        pattern[:, :, :].unsqueeze(2).to_broadcast([P, 2, 2, 4 * RANK]),
                        onehot[:, first:first + 2].unsqueeze(1).unsqueeze(3).to_broadcast([P, 2, 2, 4 * RANK]),
                        ALU.mult).then_inc(sel_done, 1)

            def select(half, t):
                g = half * TILES + t
                selectors(half, t, (2, 3))
                if g == 0:
                    for s in range(2):
                        dve.wait_ge(b_out[s], 4 * 16)
                if half:
                    dve.wait_ge(bdown_mm, (half - 1) * HPAIRS + TP * (t + 1))
                dve.wait_ge(sel_mm, (g + 1) * TP)
                for m, psum in enumerate(tile_banks(t)[2]):
                    dve.tensor_tensor(
                        u[:, m, t * TOK:(t + 1) * TOK].rearrange("p (j s c) -> p j s c", j=TP, s=2),
                        psum[:, :].rearrange("p (j s c) -> p j s c", j=TP, s=2),
                        half_mask[:, :].unsqueeze(1).unsqueeze(3).to_broadcast([P, TP, 2, C]),
                        ALU.mult).then_inc(u_done, 1)

            def opening(events):
                for what, m in events:
                    if what == "comb_in":
                        comb_in(m)
                    elif what == "comb_out":
                        comb_out(m, TP)
                    elif what == "b":
                        dve.wait_ge(b_hi_done, m + 1)
                        dve.tensor_tensor(b_parts[m][1], b_raws[m], b_parts[m][0], ALU.subtract
                                          ).then_inc(b_lo_done, 1)
                        if m == BCH - 1:
                            dve.wait_ge(b_lo_done, BCH)
                            dve.memset(vacc[:, :], 0.0).then_inc(v_zero, 1)
                    elif what == "x":
                        for j in (0, 2):
                            q = m * TP + j
                            hi, lo = layer_in(j, True)
                            dve.wait_ge(lx_hi, q + 1)
                            dve.tensor_tensor(lo, acc[:, q, :], hi, ALU.subtract).then_inc(lx_lo_v, 1)
                    elif what == "layer":
                        for j in range(TP):
                            q = m * TP + j
                            if q % 2:
                                dve.wait_ge(lx_lo_p, lows(q))
                            add_layer(q, acc[:, q, :], layer_bank[j], bias[:, q:q + 1])
                    elif what == "w":
                        for c in range(ACH if m == ADAPTERS_IN else NCH):
                            w_low(0, m, c, 1 if m == ADAPTERS_IN else 0)
                    elif what == "transpose":
                        transpose(0, m)
                    elif what == "products":
                        products(0, m)
                    elif what == "select":
                        select(0, m)

            dve.wait_ge(consts, 2)
            p0 = p_int[:, 0:1]
            link(dve.tensor_scalar(p_int[:, 5:6], p0, 6, None, ALU.logical_shift_right))
            link(dve.tensor_copy(half_mask[:, 1:2], p_int[:, 5:6]))
            link(dve.tensor_scalar(half_mask[:, 0:1], half_mask[:, 1:2], -1.0, 1.0, ALU.mult, ALU.add))

            def numbers():
                dve.tensor_scalar(p_int[:, 1:2], p0, 4, None, ALU.logical_shift_right)
                dve.tensor_scalar(p_int[:, 2:3], p0, 63, None, ALU.bitwise_and)
                dve.tensor_scalar(p_int[:, 3:4], p0, 5, 1, ALU.logical_shift_right, ALU.bitwise_and)
                dve.tensor_scalar(r_int2[:, :], r_int[:, :], 15, None, ALU.bitwise_and)
                link(dve.tensor_scalar(p_int[:, 4:5], p0, 15, None, ALU.bitwise_and))
                dve.tensor_copy(p_f[:, 0:1], p_int[:, 1:2])
                dve.tensor_copy(p_f[:, 1:2], p_int[:, 2:3])
                link(dve.tensor_scalar(p_f[:, 2:3], p_int[:, 3:4], float(P), None, ALU.mult))
                link(dve.tensor_tensor(p_f[:, 3:4], p_f[:, 2:3], p_int[:, 4:5], ALU.add))
                link(dve.tensor_scalar(p_f[:, 2:3], p_f[:, 3:4], float(BLOCKS), None, ALU.mult))
                dve.wait_ge(ints_in, 4 * 16)
                for s in range(2):
                    rows = slice(s * C, (s + 1) * C)
                    by_pair = ints[rows, :, :].rearrange("p k (q s) -> p k q s", s=2)
                    dve.tensor_copy(pair_su[rows, :], by_pair[:, 0, :, s])
                    dve.tensor_copy(pair_ad[rows, :], by_pair[:, 1, :, s])
                link(dve.tensor_copy(adf[:, :], ints[:, 1, :]))
                dve.tensor_scalar(idx_w[:, :, 0], pair_su[:, :], float(C), p_f[:, 1:2], ALU.mult, ALU.add)
                dve.tensor_scalar(idx_w[:, :, 1], pair_ad[:, :], float(C), p_f[:, 1:2], ALU.mult, ALU.add)
                dve.tensor_scalar(idx_b0[:, :], pair_ad[:, :], float(RANK * BLOCKS), p_f[:, 2:3],
                                  ALU.mult, ALU.add).then_inc(idx_done, 1)

            def tables():
                link(dve.memset(pattern[:, :, :], 0.0))
                for part in range(2):
                    for term in (part, part + 2):
                        dve.tensor_scalar(pattern[:, part, term * RANK:(term + 1) * RANK], r_int2[:, :],
                                          0.0, None, ALU.is_equal)
                link(dve.tensor_scalar(onehot[:, :], adf[:, :], p_f[:, 0:1], None, ALU.is_equal))
                for a in range(ADAPTERS):
                    link(dve.tensor_scalar((bias_n if a else bias)[:, :], pair_ad[:, :], float(a),
                                           bias_src[:, a:a + 1], ALU.is_equal, ALU.mult))
                    if a:
                        link(dve.tensor_tensor(bias[:, :], bias[:, :], bias_n[:, :], ALU.add))

            def step_h(n, slot, first=False):
                dve.wait_ge(up_mm, n + 1)
                dve.wait_ge(silu_done, silus(n + 1))
                if not first:
                    dve.wait_ge(h_lo_done, n)
                dve.tensor_tensor(h[:, :], silu[:, :], pu[slot][:, :], ALU.mult).then_inc(h_done, 1)

            def v_low(half, t):
                cols = slice(t * TOK, (t + 1) * TOK)
                dve.wait_ge(v_hi_done, half * TILES + t + 1)
                dve.tensor_tensor(u[:, 1, cols], vacc[:, cols], u[:, 0, cols], ALU.subtract).then_inc(v_done, 1)

            def v_mask(half, t):
                cols = slice(t * TOK, (t + 1) * TOK)
                first = 2 * (half * HPAIRS + t * TP)
                dve.wait_ge(down_add, adds(((half + 1) * STEPS - TILES + t + 1) * DB))
                v3 = vacc[:, cols].rearrange("p (s c) -> p s c", c=C)
                dve.tensor_tensor(
                    v3, v3, onehot[:, first:first + 2 * TP].unsqueeze(2).to_broadcast([P, 2 * TP, C]),
                    ALU.mult).then_inc(v_masked, 1)

            def finish(half, t):
                for j in range(TP):
                    q = t * TP + j
                    dve.wait_ge(bdown_mm, half * HPAIRS + q + 1)
                    dve.tensor_tensor(acc[:, q, :], pd[q % 2][:, :], acc[:, q, :], ALU.add).then_inc(y_add, 1)

            def body(half, i, last):
                first = isinstance(i, int) and i == 0
                for k in range(BODY):
                    n = i * BODY + (half * STEPS + k)
                    c, slot = k % TILES, k // TILES
                    blk = i * 2 + slot
                    if last and k > TILES:
                        v_low(half, k - TILES - 1)
                    prepares = first and k + 2 < TILES
                    if prepares:
                        transpose(half, k + 2)
                        products(half, k + 2)
                    if not (last and k == BODY - 1):
                        step_h(n + 1, (k + 1) % 2)
                    if prepares:
                        select(half, k + 2)
                    for b in range(DB):
                        dve.wait_ge(down_mm, downs(n * DB + (b + 1)))
                        if b == 2:
                            dst, psum = vacc[:, c * TOK:(c + 1) * TOK], pv
                        else:
                            j = b if b < 2 else b - 1
                            dst, psum = acc[:, c * TP + j, :], pd[j % 2]
                        dve.tensor_tensor(dst, psum[:, :], dst, ALU.add).then_inc(down_add, 1)
                    if last and slot == 1:
                        v_mask(half, c)
                    if half == 0 and first and k == 0:
                        for j in range(TP):
                            q = (TILES - 1) * TP + j
                            if q % 2:
                                dve.wait_ge(lx_lo_p, lows(q))
                            add_layer(q, acc[:, q, :], layer_bank[j], bias[:, q:q + 1])
                    if first and slot == 0:
                        for ch in FIRST_BLOCK[k]:
                            w_low(half, 1, ch, 1)
                    elif not last or slot == 0:
                        w_low(half, blk + 1, c, 1 - slot)
                    elif half + 1 < HALVES:
                        w_low(half + 1, 0, c, 0)
                    if last and k > TILES:
                        finish(half, k - TILES - 1)
                    if half == 0:
                        q = i * 2 + (HPAIRS + slot)
                        e = comb(q)
                        if c == 1:
                            comb_in_one(e)
                        elif c == 2:
                            comb_out(e, 1)
                        elif c == 3:
                            dve.wait_ge(lx_lo_p, lows(q))
                            add_layer(q, xn[:, slot, :], px,
                                      bias[:, q:q + 1] if isinstance(q, int) else bias[:, bass.ds(q, 1)])

            opening(OPENING[:2])
            tables()
            opening(OPENING[2:])
            dve.wait_ge(bdn_hi_done, 1)
            dve.tensor_tensor(bdn_lo[:, :], silu[:, :], bdn_hi[:, :], ALU.subtract).then_inc(bdn_done, 1)
            dve.sem_inc(h_done, 1)
            dve.sem_inc(down_add, 1)
            for half in range(HALVES):
                if half:
                    for c in range(ACH):
                        w_low(half, ADAPTERS_IN, c, 1)
                    transpose(half, 0)
                    v_low(half - 1, TILES - 1)
                    products(half, 0)
                    finish(half - 1, TILES - 1)
                    select(half, 0)
                transpose(half, 1)
                products(half, 1)
                step_h(half * STEPS, 0, first=half == 0)
                select(half, 1)
                if half == 0:
                    opening(AFTER_FIRST)
                dve.wait_ge(v_zero, 1 + half * TILES)
                body(half, 0, False)
                with dve.Fori(1, TURNS - 1) as i:
                    body(half, i, False)
                body(half, TURNS - 1, True)
            v_low(HALVES - 1, TILES - 1)
            finish(HALVES - 1, TILES - 1)

        @block.tensor
        def _(pe):
            def split_product(psum, w_parts, x_parts, chunks=1, close=True, fresh=True):
                done = 0
                for c in range(chunks):
                    for wi, xi in ((0, 0), (0, 1), (1, 0)):
                        ins = pe.matmul(psum, w_parts[wi](c), x_parts[xi](c), start=(fresh and done == 0),
                                        stop=(close and done == 3 * chunks - 1))
                        done += 1
                return ins

            def combine(e, n):
                pe.wait_ge(e_lo_done, e + 1)
                for j in range(n):
                    ins = split_product(px[:, j * C:(j + 1) * C],
                                        [lambda c, w=w: w[:, j, :] for w in (et_hi, et_lo)],
                                        [lambda c, w=w: w[:, j, :] for w in (eb_hi, eb_lo)])
                ins.then_inc(e_mm, 1)

            def layer(q, j, psum, first_half):
                hi, lo = layer_in(j, first_half)
                pe.wait_ge(lx_lo_v if first_half and q % 2 == 0 else lx_lo_p, lows(q))
                split_product(psum[:, :], [lambda c: bd_hi[:, j, :], lambda c: bd_lo[:, j, :]],
                              [lambda c: hi, lambda c: lo]).then_inc(layer_mm, 1)

            def layers(t):
                pe.wait_ge(bd_done, t + 1)
                for j in range(TP):
                    layer(t * TP + j, j, layer_bank[j], True)

            def transpose(half, t):
                g = half * TILES + t
                if half == 0:
                    pe.wait_ge(layer_add, (t + 1) * TP)
                else:
                    pe.wait_ge(x3_in[t], 16)
                for c, psum in enumerate(tile_banks(t)[0]):
                    for j in range(TP):
                        ins = pe.transpose(psum[:, j * P:(j + 1) * P],
                                           acc[:, t * TP + j, c * P:(c + 1) * P], ident[:, :])
                    ins.then_inc(tr_mm, 1)

            def products(half, t):
                g = half * TILES + t
                cols = slice(t * TOK, (t + 1) * TOK)
                pe.wait_ge(xt_done, (g + 1) * KC)
                pe.wait_ge(w_done, conv(half, ADAPTERS_IN, ACH - 1))
                for m, psum in enumerate(tile_banks(t)[1]):
                    split_product(psum[:, :],
                                  [lambda c, w=w: w[:, 1, (m * KC + c) * P:(m * KC + c + 1) * P]
                                   for w in (w_hi, w_lo)],
                                  [lambda c, s=s: s[:, c, cols] for s in (xt_hi, xt_lo)],
                                  chunks=KC).then_inc(a_mm, 1)

            def select(half, t):
                g = half * TILES + t
                pe.wait_ge(ua_done, (g + 1) * 2)
                for j in range(TP):
                    pe.wait_ge(sel_done, g * TP + j + 1)
                    for m, psum in enumerate(tile_banks(t)[2]):
                        for part in range(2):
                            ins = pe.matmul(psum[:, j * P:(j + 1) * P],
                                            sel[:, j % 2, part].rearrange("p s e -> p (s e)"),
                                            ua_parts[m][part][:, j * P:(j + 1) * P],
                                            start=(part == 0), stop=(part == 1))
                    ins.then_inc(sel_mm, 1)

            def hidden(half, m, n, t, wslot, slot, blk, loads):
                psum, base, done = ((pg[slot], GATE, gate_mm), (pu[slot], UP, up_mm))[m]
                cols = slice(t * TOK, (t + 1) * TOK)
                pe.wait_ge(w_done, conv(half, blk, m))
                if not (isinstance(n, int) and n % STEPS == 0):
                    pe.wait_ge(*((silu_done, silus(n - 1)), (h_done, hs(n - 1)))[m])
                split_product(psum[:, :],
                              [lambda c, w=w: w[:, wslot, base + c * P:base + (c + 1) * P] for w in (w_hi, w_lo)],
                              [lambda c, s=s: s[:, c, cols] for s in (xt_hi, xt_lo)],
                              chunks=KC, close=False)
                if m == 0:
                    pe.wait_ge(b_got_in[slot], loads)
                for j in range(TP):
                    ins = pe.matmul(psum[:, j * P:(j + 1) * P], b_got[:, slot, j, m * P:(m + 1) * P],
                                    u[:, m, t * TOK + j * P:t * TOK + (j + 1) * P],
                                    start=False, stop=(j == TP - 1))
                ins.then_inc(done, 1)

            def down(half, n, wslot, slot, blk, selections=0):
                pe.wait_ge(h_lo_done, n + 1)
                pe.wait_ge(w_done, conv(half, blk, NCH - 1))
                for b in range(DB):
                    if b == 0:
                        pe.wait_ge(down_add, adds(n * DB))
                    elif b > 2:
                        pe.wait_ge(down_add, adds(n * DB + (b - 2)))
                    if b == 2:
                        if selections:
                            pe.wait_ge(u_done, selections)
                        ins = split_product(pv[:, :],
                                            [lambda c, w=w: w[:, wslot, ADOWN:ADOWN + P] for w in (w_hi, w_lo)],
                                            [lambda c, s=s: s[:, slot, :] for s in (h_hi, h_lo)])
                    else:
                        j = b if b < 2 else b - 1
                        ins = split_product(pd[j % 2][:, :],
                                            [lambda c, s=s: s[:, slot, j * P:(j + 1) * P] for s in (h_hi, h_lo)],
                                            [lambda c, w=w: w[:, wslot, DOWN:DOWN + T] for w in (w_hi, w_lo)])
                    ins.then_inc(down_mm, 1)

            def finish(half, t):
                pe.wait_ge(v_done, half * TILES + t + 1)
                for j in range(TP):
                    q = t * TP + j
                    if j >= 2:
                        pe.wait_ge(y_add, half * HPAIRS + q - 1)
                    split_product(pd[q % 2][:, :],
                                  [lambda c, m=m: u[:, m, q * P:(q + 1) * P] for m in range(2)],
                                  [lambda c, w=w: w[:, :] for w in (bdn_hi, bdn_lo)]
                                  ).then_inc(bdown_mm, 1)

            def opening(events):
                for what, m in events:
                    if what == "comb_out":
                        if m:
                            pe.wait_ge(e_add, m)
                        if m >= 2:
                            pe.wait_ge(layer_add, (m - 1) * TP)
                        if m == TILES:
                            pe.wait_ge(u_done, 2 * 2)
                        combine(m, TP)
                    elif what == "layer":
                        if m >= 2:
                            pe.wait_ge(u_done, m * 2)
                        layers(m)
                    elif what == "transpose":
                        transpose(0, m)
                    elif what == "products":
                        products(0, m)
                    elif what == "select":
                        select(0, m)

            def body(half, i, last):
                first = isinstance(i, int) and i == 0
                g0 = half * TILES
                for k in range(BODY):
                    n = i * BODY + (half * STEPS + k)
                    c, slot = k % TILES, k // TILES
                    blk = i * 2 + slot
                    m = k + 1
                    nxt = (half, n + 1, m % TILES, (m // TILES) % 2, m % 2, i * 2 + m // TILES,
                           i * (BODY * TP * 8) + ((half * STEPS + m) // 2 + 1) * TP * 16)
                    prepares = first and k + 2 < TILES
                    if prepares:
                        pe.wait_ge(u_done, (g0 + k + 2) * 2)
                        if k:
                            pe.wait_ge(down_add, adds(n * DB))
                        if half == 0 and k == 0:
                            pe.wait_ge(e_add, TILES + 1)
                        transpose(half, k + 2)
                    if not (last and k == BODY - 1):
                        hidden(nxt[0], 0, *nxt[1:])
                    if prepares:
                        products(half, k + 2)
                    if not (last and k == BODY - 1):
                        hidden(nxt[0], 1, *nxt[1:])
                    if prepares:
                        select(half, k + 2)
                    if last and k > TILES + 1:
                        pe.wait_ge(y_add, half * HPAIRS + TP * (k - TILES - 1))
                    down(half, n, slot, k % 2, blk, (g0 + k + 3) * 2 if prepares else 0)
                    if half == 0 and first and k == 0:
                        pe.wait_ge(down_add, adds(DB))
                        layers(TILES - 1)
                    if last and k > TILES:
                        pe.wait_ge(down_add, adds((n + 1) * DB))
                        finish(half, k - TILES - 1)
                    if half == 0:
                        q = i * 2 + (HPAIRS + slot)
                        if c == 2:
                            pe.wait_ge(layer_add, q)
                            combine(comb(q), 1)
                        elif c == 3:
                            pe.wait_ge(e_add, comb(q) + 1)
                            pe.wait_ge(bd_done, comb(q))
                            layer(q, 0, px, False)

            pe.wait_ge(consts, 3)
            opening(OPENING)
            pe.sem_inc(down_mm, 1)
            for half in range(HALVES):
                g0 = half * TILES
                if half:
                    pe.wait_ge(silu_done, silus(half * STEPS))
                    pe.wait_ge(h_done, hs(half * STEPS))
                    transpose(half, 0)
                    products(half, 0)
                    pe.wait_ge(y_add, half * HPAIRS - TP)
                    finish(half - 1, TILES - 1)
                    select(half, 0)
                    pe.wait_ge(y_add, half * HPAIRS)
                    pe.wait_ge(layer_add, PAIRS)
                pe.wait_ge(u_done, (g0 + 1) * 2)
                if half == 0:
                    pe.wait_ge(e_add, TILES)
                n0 = half * STEPS
                first = (half, n0, 0, 0, 0, 0, (n0 // 2 + 1) * TP * 16)
                transpose(half, 1)
                hidden(first[0], 0, *first[1:])
                products(half, 1)
                hidden(first[0], 1, *first[1:])
                select(half, 1)
                if half == 0:
                    opening(AFTER_FIRST)
                body(half, 0, False)
                with pe.Fori(1, TURNS - 1) as i:
                    body(half, i, False)
                body(half, TURNS - 1, True)
            pe.wait_ge(y_add, HALVES * HPAIRS - TP)
            finish(HALVES - 1, TILES - 1)


def kernel(x, itok_B_1_198, itok_B_0_7, fside_8xS_0, L0_cond_weights, L1_cond_weights, L2_cond_weights,
           L3_cond_Wg, L3_cond_Wu, L3_cond_Wd, L3_cond_Ag, L3_cond_Bg, L3_cond_Au, L3_cond_Bu,
           L3_cond_Ad, L3_cond_Bd):
    import numpy as np
    import concourse.bacc as bacc
    from concourse.bass_utils import run_bass_kernel_spmd

    def a(v):
        return np.asarray(v)

    def by_block(w):
        return a(w).reshape(KC, P, BLOCKS, P).transpose(2, 1, 0, 3).reshape(BLOCKS, P, KC * P)

    def adapters_in(w):
        return a(w).reshape(ADAPTERS, KC, P, RANK).transpose(2, 1, 0, 3).reshape(P, KC * P)

    def adapters_out(w):
        return a(w).reshape(P, BLOCKS, 1, P)

    def with_transposed(w):
        return np.concatenate([a(w), a(w).transpose(0, 2, 1)], axis=2).reshape(-1, 2 * C)

    arrays = {
        "x": a(x),
        "subject": a(itok_B_1_198),
        "adapter": a(itok_B_0_7),
        "w0_rows": with_transposed(L0_cond_weights),
        "w1_rows": with_transposed(L1_cond_weights),
        "w2_rows": a(L2_cond_weights).reshape(-1, C),
        "bias_t": a(fside_8xS_0).T,
        "w_all": np.concatenate(
            [by_block(L3_cond_Wg), by_block(L3_cond_Wu), a(L3_cond_Wd).reshape(BLOCKS, P, T),
             a(L3_cond_Ad).reshape(ADAPTERS, BLOCKS, P, RANK).transpose(1, 2, 0, 3).reshape(BLOCKS, P, P)],
            axis=2),
        "a_all": np.concatenate([adapters_in(L3_cond_Ag), adapters_in(L3_cond_Au)], axis=1),
        "b_rows": np.concatenate([adapters_out(L3_cond_Bg), adapters_out(L3_cond_Bu)], axis=2).reshape(P, -1),
        "bd_rows": a(L3_cond_Bd).reshape(P, T),
    }
    arrays = {name: np.ascontiguousarray(v) for name, v in arrays.items()}

    nc = bacc.Bacc("TRN2", target_bir_lowering=False, num_devices=1)
    t = {name: nc.dram_tensor(name, v.shape, mybir.dt.from_np(v.dtype), kind="ExternalInput").ap()
         for name, v in arrays.items()}
    out = nc.dram_tensor("out", (SAMPLES, C, T), F32, kind="ExternalOutput").ap()
    cond_resid_kernel(nc, t["x"], t["subject"], t["adapter"], t["w0_rows"], t["w1_rows"], t["w2_rows"],
                      t["bias_t"], t["w_all"], t["a_all"], t["b_rows"], t["bd_rows"], out)
    r = run_bass_kernel_spmd(nc, [arrays], core_ids=[0])
    return r.results[0]["out"]
```

```python
from contextlib import ExitStack

import concourse.bass as bass
from concourse import mybir

F32 = mybir.dt.float32
F32R = mybir.dt.float32r
I32 = mybir.dt.int32
U32 = mybir.dt.uint32
ALU = mybir.AluOpType
ACT = mybir.ActivationFunctionType

P = 128
SAMPLES, C, T = 64, 64, 512
ADAPTERS, RANK = 8, 16
HIDDEN = 2048
KC = T // P
BLOCKS = HIDDEN // P
PAIRS = SAMPLES // 2
HALVES = 2
HPAIRS = PAIRS // HALVES
TP = 4
TILES = HPAIRS // TP
TOK = TP * P
STEPS = BLOCKS * TILES
BODY = 2 * TILES
TURNS = STEPS // BODY

CHUNKS = ((0, 512), (512, 1024), (1024, 1536), (1536, 1664))
WCOLS = CHUNKS[-1][1]
GATE, UP, DOWN, ADOWN = (lo for lo, _ in CHUNKS)
NCH = len(CHUNKS)
ACH = 2
ADAPTERS_IN = -1
WARM_UP = (10, 12, 7)
FIRST_BLOCK = ((), (), (0, 1), (2, 3))
CONV = ACH + NCH * BLOCKS
DB = TP + 1
BCH = 4
BCOLS = BLOCKS * 2 * P // BCH


def cond_resid_kernel(nc, x, subject, adapter, w0_rows, w1_rows, w2_rows, bias_t, w_all, a_all, b_rows, bd_rows, out):
    b_table = nc.dram_tensor("b_table", (2 * P * BLOCKS, 2 * P), F32).ap()
    b_first = nc.dram_tensor("b_first", (2 * P, 2 * P), F32).ap()
    e_table = nc.dram_tensor("e_table", (ADAPTERS * C, C), F32).ap()
    x3_next = nc.dram_tensor("x3_next", (HPAIRS, P, T), F32).ap()

    with ExitStack() as ctx:
        def sb(name, shape, dt=F32):
            return ctx.enter_context(nc.sbuf_tensor(name, shape, dt))

        def bank(name):
            return ctx.enter_context(nc.psum_tensor(name, [P, 512], F32))

        def sem(name):
            return ctx.enter_context(nc.semaphore(name))

        xt_hi = sb("xt_hi", [P, KC, TILES * TOK], F32R)
        xt_lo = sb("xt_lo", [P, KC, TILES * TOK], F32R)
        acc = sb("acc", [P, HPAIRS, T])
        u = sb("u", [P, 2, TILES * TOK], F32R)
        vacc = sb("vacc", [P, TILES * TOK])
        w_raw = sb("w_raw", [P, WCOLS])
        w_hi = sb("w_hi", [P, 2, WCOLS], F32R)
        w_lo = sb("w_lo", [P, 2, WCOLS], F32R)
        b_got = sb("b_got", [P, 2, TP, 2 * P], F32R)
        silu = sb("silu", [P, TOK])
        h = sb("h", [P, TOK])
        h_hi = sb("h_hi", [P, 2, TOK], F32R)
        h_lo = sb("h_lo", [P, 2, TOK], F32R)
        xn = sb("xn", [P, 2, T])
        xn_hi = sb("xn_hi", [P, T], F32R)
        xn_lo = sb("xn_lo", [P, T], F32R)
        ya_hi = sb("ya_hi", [P, T], F32R)
        ya_lo = sb("ya_lo", [P, T], F32R)
        et_hi = sb("et_hi", [P, TP, P], F32R)
        et_lo = sb("et_lo", [P, TP, P], F32R)
        eb_hi = sb("eb_hi", [P, TP, C], F32R)
        eb_lo = sb("eb_lo", [P, TP, C], F32R)
        eb_raw = sb("eb_raw", [P, TP, C])
        e_sum = sb("e_sum", [P, TP, C])
        ea_one = sb("ea_one", [P, 1, P])
        eb_one = sb("eb_one", [P, 1, C])
        em_one = sb("em_one", [P, 1, P])
        bd_hi = sb("bd_hi", [P, TP, P], F32R)
        bd_lo = sb("bd_lo", [P, TP, P], F32R)
        bdn_hi = sb("bdn_hi", [P, T], F32R)
        bdn_lo = sb("bdn_lo", [P, T], F32R)
        ident = sb("ident", [P, P])
        pattern = sb("pattern", [P, 2, 4 * RANK])
        sel = sb("sel", [P, 2, 2, 2, 4 * RANK], F32R)
        ints = sb("ints", [P, 2, SAMPLES], I32)
        adf = sb("adf", [P, SAMPLES])
        pair_ad = sb("pair_ad", [P, PAIRS])
        pair_su = sb("pair_su", [P, PAIRS])
        onehot = sb("onehot", [P, SAMPLES])
        bias = sb("bias", [P, PAIRS])
        bias_n = sb("bias_n", [P, PAIRS])
        bias_src = sb("bias_src", [P, ADAPTERS])
        p_int = sb("p_int", [P, 8], I32)
        p_f = sb("p_f", [P, 4])
        half_mask = sb("half_mask", [P, 2])
        r_int = sb("r_int", [P, RANK], I32)
        r_int2 = sb("r_int2", [P, RANK], I32)
        idx_w = sb("idx_w", [P, PAIRS, 2], I32)
        idx_f = sb("idx_f", [P, PAIRS], I32)
        idx_b0 = sb("idx_b0", [P, PAIRS], I32)
        idx_b = sb("idx_b", [P, 2, PAIRS], I32)
        idx_now = sb("idx_now", [P, 2], I32)

        pg = [bank(f"pg{i}") for i in range(2)]
        pu = [bank(f"pu{i}") for i in range(2)]
        pd = [bank(f"pd{i}") for i in range(2)]
        pv = bank("pv")
        px = bank("px")
        layer_bank = [pd[0], pd[1], px, pv]

        def four(ap):
            return ap.rearrange("p (j n) -> p j n", j=TP)

        ea_four = [four(a) for a in (xn[:, 0, :], acc[:, 12, :], acc[:, 13, :], acc[:, 14, :], xn[:, 0, :])]
        eb_four = [eb_raw[:, :, :], four(acc[:, 15, 0:TP * C]), four(acc[:, 15, TP * C:2 * TP * C]),
                   four(h_hi[:, 1, 0:TP * C].bitcast(F32)), eb_raw[:, :, :]]
        em_four = four(xn[:, 1, :])
        b_raws = [vacc[:, 0:BCOLS], vacc[:, BCOLS:2 * BCOLS],
                  acc[:, 8:10, :].rearrange("p j n -> p (j n)"), acc[:, 10:12, :].rearrange("p j n -> p (j n)")]
        b_parts = [[u[:, part, j * BCOLS:(j + 1) * BCOLS] for part in range(2)] for j in range(2)] \
            + [[xt[:, j, TOK:TOK + BCOLS] for xt in (xt_hi, xt_lo)] for j in range(2)]

        ints_in = sem("ints_in")
        e0_in = sem("e0_in")
        x_in = [sem(f"x_in{t}") for t in range(TILES)]
        b_in = [sem(f"b_in{i}") for i in range(BCH)]
        bdn_in = sem("bdn_in")
        raw_in = [sem(f"raw_in{c}") for c in range(NCH)]
        b_out = [sem(f"b_out{i}") for i in range(BCH)]
        b_first_out = sem("b_first_out")
        e_out = sem("e_out")
        x3_out = [sem(f"x3_out{i}") for i in range(2)]
        x3_in = [sem(f"x3_in{t}") for t in range(TILES)]
        xn_in = [sem(f"xn_in{i}") for i in range(2)]
        y_out = [sem(f"y_out{t}") for t in range(TILES)]
        e_in = sem("e_in")
        e_tile_in = [sem(f"e_tile_in{t}") for t in range(TILES)]
        b_got_in = [sem(f"b_got_in{i}") for i in range(2)]
        consts = sem("consts")
        pool_step = sem("pool_step")
        dve_step = sem("dve_step")
        idx_done = sem("idx_done")
        b_hi_done = sem("b_hi_done")
        b_lo_done = sem("b_lo_done")
        bdn_done = sem("bdn_done")
        bdn_hi_done = sem("bdn_hi_done")
        e_t_done = sem("e_t_done")
        e_hi_done = sem("e_hi_done")
        e_lo_done = sem("e_lo_done")
        e_sum_done = sem("e_sum_done")
        e_mm = sem("e_mm")
        e_add = sem("e_add")
        e_masked = sem("e_masked")
        bd_hi_done = sem("bd_hi_done")
        bd_done = sem("bd_done")
        lx_hi = sem("lx_hi")
        lx_lo_p = sem("lx_lo_p")
        lx_lo_v = sem("lx_lo_v")
        layer_mm = sem("layer_mm")
        layer_add = sem("layer_add")
        tr_mm = sem("tr_mm")
        xt_hi_done = sem("xt_hi_done")
        xt_done = sem("xt_done")
        a_mm = sem("a_mm")
        ua_hi = sem("ua_hi")
        ua_done = sem("ua_done")
        sel_done = sem("sel_done")
        sel_mm = sem("sel_mm")
        u_done = sem("u_done")
        v_zero = sem("v_zero")
        w_hi_done = sem("w_hi_done")
        w_done = sem("w_done")
        gate_mm = sem("gate_mm")
        up_mm = sem("up_mm")
        silu_done = sem("silu_done")
        h_done = sem("h_done")
        h_hi_done = sem("h_hi_done")
        h_lo_done = sem("h_lo_done")
        down_mm = sem("down_mm")
        down_add = sem("down_add")
        v_masked = sem("v_masked")
        v_hi_done = sem("v_hi_done")
        v_done = sem("v_done")
        bdown_mm = sem("bdown_mm")
        y_add = sem("y_add")
        idx_next = sem("idx_next")
        may_gather = sem("may_gather")

        block = ctx.enter_context(nc.Block())

        def conv(half, blk, c):
            if isinstance(blk, int) and blk == ADAPTERS_IN:
                return CONV * half + NCH + c + 1
            if isinstance(blk, int) and blk == 0:
                return CONV * half + c + 1
            return blk * NCH + (CONV * half + ACH + c + 1)

        def raw_loads(half, blk, c):
            if c >= ACH:
                return blk + (BLOCKS * half + 1)
            if isinstance(blk, int) and blk <= 0:
                return (BLOCKS + 1) * half + (2 if blk == ADAPTERS_IN else 1)
            return blk + ((BLOCKS + 1) * half + 2)

        def silus(n): return n + 1
        def hs(n): return n + 1
        def downs(n): return n + 1
        def adds(n): return n + 1

        def comb(q):
            return q + (TILES + 1 - HPAIRS)

        def layer_in(j, first_half):
            if first_half:
                tail = slice((TILES - 1) * TOK, TILES * TOK)
                return xt_hi[:, j, tail], xt_lo[:, j, tail]
            return xn_hi[:, :], xn_lo[:, :]

        def lows(q):
            if isinstance(q, int) and q < HPAIRS:
                return q // 2 + 1
            return q + (HPAIRS // 2 - HPAIRS + 1)

        def next_half(half, c):
            if half + 1 == HALVES or c == TILES - 1:
                return []
            if c < TILES - 2:
                return [(half + 1, 0, c, 0)]
            return [(half + 1, 0, ch, 0) for ch in range(c, NCH)] \
                + [(half + 1, ADAPTERS_IN, ch, 1) for ch in range(ACH)]

        ua_parts = [(xn_hi[:, :], xn_lo[:, :]), (ya_hi[:, :], ya_lo[:, :])]

        def tile_banks(t):
            if t == 0:
                return pg + pu, pg, pu
            return [pv, px, pd[0], pd[1]], [pv, px], [px, pu[t % 2]]

        finish_banks = [pd[0], pd[1], pv, pd[0]]
        last_banks = [px, pv, pd[0], pd[1]]

        def combination_bank(e):
            return pd[0] if isinstance(e, int) and 2 < e <= TILES else px

        OPENING = (("comb_in", 0), ("comb_out", 0), ("b", 0), ("x", 0), ("w", 0), ("b", 1),
                   ("comb_in", 1), ("b", 2), ("comb_out", 1), ("w", ADAPTERS_IN), ("layer", 0), ("b", 3),
                   ("transpose", 0), ("x", 1), ("comb_in", 2), ("products", 0), ("comb_out", 2), ("select", 0))
        EARLY = TILES - 1

        @block.sync
        def _(sp):
            def load_raw(half, blk, c):
                lo, hi = CHUNKS[c]
                if not isinstance(blk, int):
                    src = w_all[bass.ds(blk, 1), :, lo:hi].rearrange("a p n -> (a p) n")
                elif blk == ADAPTERS_IN:
                    src = a_all[:, lo:hi]
                else:
                    src = w_all[blk, :, lo:hi]
                sp.dma_start(w_raw[:, lo:hi], src).then_inc(raw_in[c], 16)

            def load_x(t):
                src = x[2 * TP * t:2 * TP * (t + 1)].rearrange("(q s) c t -> (s c) q t", s=2)
                sp.dma_start(acc[:, TP * t:TP * (t + 1), :], src).then_inc(x_in[t], 16)

            def load_b(j):
                sp.dma_start(b_raws[j], b_rows[:, j * BCOLS:(j + 1) * BCOLS]).then_inc(b_in[j], 16)

            def store_b(j):
                sp.wait_ge(b_lo_done, j + 1)
                table = b_table.rearrange("(g p k) n -> g p (k n)", g=2, k=BLOCKS)
                for part in range(2):
                    sp.dma_start(table[part, :, j * BCOLS:(j + 1) * BCOLS],
                                 b_parts[j][part].bitcast(F32)).then_inc(b_out[j], 16)

            def load_xn(q, slot):
                src = (x[2 * q:2 * q + 2] if isinstance(q, int) else x[bass.ds(q * 2, 2)])
                sp.dma_start(xn[:, slot, :], src.rearrange("s c t -> (s c) t")).then_inc(xn_in[slot], 16)

            sp.dma_start(ea_four[0], w1_rows.rearrange("(j p) n -> p j n", p=P)).then_inc(e0_in, 16)
            sp.dma_start(eb_four[0], w2_rows.rearrange("(j p) n -> p j n", p=P)).then_inc(e0_in, 16)
            sp.dma_start(ints[:, 0, :], subject.partition_broadcast(P)).then_inc(ints_in, 16)
            sp.dma_start(ints[:, 1, :], adapter.partition_broadcast(P)).then_inc(ints_in, 16)
            for s in range(2):
                sp.dma_start(bias_src[s * C:(s + 1) * C, :], bias_t).then_inc(ints_in, 16)
            load_b(0)
            load_x(0)
            for c in range(NCH):
                load_raw(0, 0, c)
            sp.wait_ge(e_add, 1)
            sp.dma_start(e_table.rearrange("(j p) n -> p j n", p=P), e_sum[:, :, :]).then_inc(e_out, 16)
            load_b(1)
            load_b(2)
            sp.wait_ge(e_tile_in[0], 2 * TP * 16)
            load_b(3)
            for c in range(ACH):
                sp.wait_ge(w_done, conv(0, 0, c))
                load_raw(0, ADAPTERS_IN, c)
            sp.wait_ge(b_lo_done, 1)
            for part in range(2):
                sp.dma_start(b_first[part * P:(part + 1) * P, :], b_parts[0][part][:, 0:2 * P].bitcast(F32)
                             ).then_inc(b_first_out, 16)
            sp.dma_start(silu[:, :], bd_rows).then_inc(bdn_in, 16)
            load_x(1)
            sp.wait_ge(e_tile_in[1], 2 * TP * 16)
            for j in range(BCH):
                store_b(j)
            load_x(2)
            for c in range(ACH, NCH):
                sp.wait_ge(w_done, conv(0, 0, c))
                load_raw(0, 1, c)
            sp.wait_ge(e_sum_done, TILES)
            load_x(3)
            sp.wait_ge(bd_done, TILES)
            load_xn(HPAIRS, 0)
            load_xn(HPAIRS + 1, 1)

            def store_y(half, t):
                first = 2 * TP * (half * TILES + t)
                sp.wait_ge(y_add, half * HPAIRS + TP * (t + 1))
                sp.dma_start(out[first:first + 2 * TP].rearrange("(q s) c t -> (s c) q t", s=2),
                             acc[:, TP * t:TP * (t + 1), :]).then_inc(y_out[t], 16)

            def store_last_pairs(half):
                for q in range(HPAIRS - TP, HPAIRS):
                    first = 2 * (half * HPAIRS + q)
                    sp.wait_ge(y_add, half * HPAIRS + q + 1)
                    sp.dma_start(out[first:first + 2].rearrange("s c t -> (s c) t"), acc[:, q, :]
                                 ).then_inc(y_out[TILES - 1], 16)

            def load_x3(t):
                sp.wait_ge(y_out[t], 16)
                sp.dma_start(acc[:, TP * t:TP * (t + 1), :],
                             x3_next[TP * t:TP * (t + 1)].rearrange("q p t -> p q t")).then_inc(x3_in[t], 16)

            def after_conversion(half, i, k, last):
                blk = i * 2 + k // TILES
                if isinstance(i, int) and i == 0 and k < TILES:
                    chunks = FIRST_BLOCK[k]
                else:
                    chunks = (k % TILES,)
                for c in chunks:
                    if not last:
                        sp.wait_ge(w_done, conv(half, blk + 1, c))
                        load_raw(half, blk + 2, c)
                    elif half + 1 < HALVES:
                        if k < TILES:
                            sp.wait_ge(w_done, conv(half, blk + 1, c))
                            load_raw(half + 1, 0, c)
                        else:
                            sp.wait_ge(w_done, conv(half + 1, 0, c))
                            load_raw(half + 1, ADAPTERS_IN if c < ACH else 1, c)

            def body(half, i, last):
                for k in range(BODY):
                    blk = i * 2 + (k // TILES)
                    if last and half == 0 and k == BODY - 2:
                        for slot in range(2):
                            sp.wait_ge(x3_out[slot], TURNS * 16 - 16)
                        load_x3(0)
                    after_conversion(half, i, k, last)
                    if last and half == 0 and k == BODY - 1:
                        sp.wait_ge(x3_out[0], TURNS * 16)
                        load_x3(1)
                    if last and k >= TILES + 1:
                        store_y(half, k - TILES - 1)
                    if half == 0 and k % TILES == TILES - 1:
                        slot = k // TILES
                        q = blk + HPAIRS
                        sp.wait_ge(layer_add, q + 1)
                        if isinstance(blk, int):
                            dst = x3_next[blk]
                        else:
                            dst = x3_next[bass.ds(blk, 1)].rearrange("a p t -> (a p) t")
                        sp.dma_start(dst, xn[:, slot, :]).then_inc(x3_out[slot], 16)
                        if not last:
                            sp.wait_ge(x3_out[slot], i * 16 + 16)
                            load_xn(q + 2, slot)

            for half in range(HALVES):
                for c in range(ACH):
                    sp.wait_ge(w_done, conv(half, ADAPTERS_IN, c))
                    load_raw(half, 1, c)
                body(half, 0, False)
                with sp.Fori(1, TURNS - 1) as i:
                    body(half, i, False)
                body(half, TURNS - 1, True)
                if half == 0:
                    load_x3(TILES - 2)
                if half == 0:
                    store_y(half, TILES - 1)
                else:
                    store_last_pairs(half)
                if half == 0:
                    sp.wait_ge(x3_out[1], TURNS * 16)
                    load_x3(TILES - 1)
            for t in range(TILES):
                sp.wait_ge(y_out[t], (2 if t < TILES - 1 else 1 + TP) * 16)
            for j in range(BCH):
                sp.wait_ge(b_out[j], 2 * 16)
            sp.wait_ge(b_first_out, 2 * 16)
            sp.wait_ge(e_out, 16)

        @block.gpsimd
        def _(gp):
            chain = [0]

            def link(ins):
                chain[0] += 1
                ins.then_inc(pool_step, 1)
                gp.wait_ge(pool_step, chain[0])

            gp.iota(p_int[:, 0:1], [[0, 1]], base=0, channel_multiplier=1).then_inc(consts, 1)
            gp.iota(r_int[:, :], [[1, RANK]], base=P, channel_multiplier=-1).then_inc(consts, 1)
            link(gp.memset(ident[:, :], 0.0))
            gp.affine_select(out=ident[:, :], in_=ident[:, :], compare_op=ALU.not_equal, fill=1.0, base=0,
                             pattern=[[-1, P]], channel_multiplier=1).then_inc(consts, 1)

            def wait_before_gather(semaphore, value):
                gp.wait_ge(semaphore, value)
                gp.sem_inc(may_gather, 1)

            def gather_rows(dst, table, rows, semaphore):
                gp.indirect_dma_start(out=dst, out_offset=None, in_=table,
                                      in_offset=bass.IndirectOffsetOnAxis(ap=rows.bitcast(U32), axis=0)
                                      ).then_inc(semaphore, 16)

            def gather_tile(e):
                gp.wait_ge(idx_done, 1)
                gp.wait_ge(e_sum_done, 1)
                for j in range(TP):
                    q = (e - 1) * TP + j
                    gather_rows(ea_four[e][:, j, :], w0_rows, idx_w[:, q, 0:1], e_tile_in[e - 1])
                gp.wait_ge(e_out, 16)
                for j in range(TP):
                    q = (e - 1) * TP + j
                    gather_rows(eb_four[e][:, j, :], e_table, idx_w[:, q, 1:2], e_tile_in[e - 1])

            def gather_b(half, m, parity, slot, first=False):
                for j in range(TP):
                    q = half * HPAIRS + (m % TILES) * TP + j
                    gather_rows(b_got[:, slot, j, :].bitcast(F32), b_first if first else b_table,
                                idx_f[:, q:q + 1] if first else idx_b[:, parity, q:q + 1], b_got_in[slot])

            def comb_in(e):
                gp.wait_ge(e_hi_done, e + 1)
                gp.tensor_tensor(et_lo[:, 0:1, :], em_one[:, :, :], et_hi[:, 0:1, :], ALU.subtract)
                gp.tensor_tensor(eb_lo[:, 0:1, :], eb_one[:, :, :], eb_hi[:, 0:1, :], ALU.subtract
                                 ).then_inc(e_lo_done, 1)
                gp.wait_ge(e_masked, e - 1)
                gp.tensor_tensor(e_sum[:, 0:1, :], ea_one[:, :, 0:C], eb_one[:, :, :], ALU.add
                                 ).then_inc(e_sum_done, 1)

            def comb_out(e):
                gp.wait_ge(bd_hi_done, e)
                gp.tensor_tensor(bd_lo[:, 0:1, :], em_one[:, :, :], bd_hi[:, 0:1, :], ALU.subtract
                                 ).then_inc(bd_done, 1)

            def split_x(q, j, source, first_half):
                hi, lo = layer_in(j, first_half)
                gp.wait_ge(lx_hi, q + 1)
                gp.tensor_tensor(lo, source, hi, ALU.subtract).then_inc(lx_lo_p, 1)

            def next_block(parity, count):
                gp.tensor_scalar(idx_b[:, parity, :], idx_b[:, 1 - parity, :], 1.0, None, ALU.add
                                 ).then_inc(idx_next, 1)
                wait_before_gather(idx_next, count)

            def split_odd(t):
                for j in (1, 3):
                    split_x(t * TP + j, j, acc[:, t * TP + j, :], True)

            def step_lo(slot, n):
                gp.wait_ge(h_hi_done, n + 1)
                gp.tensor_tensor(h_lo[:, slot, :], h[:, :], h_hi[:, slot, :], ALU.subtract
                                 ).then_inc(h_lo_done, 1)

            def w_low(half, blk, c, slot):
                lo, hi = CHUNKS[c]
                gp.wait_ge(w_hi_done, conv(half, blk, c))
                gp.wait_ge(w_done, conv(half, blk, c) - 1)
                gp.tensor_tensor(w_lo[:, slot, lo:hi], w_raw[:, lo:hi], w_hi[:, slot, lo:hi],
                                 ALU.subtract).then_inc(w_done, 1)

            def half_start(half):
                if half == 0:
                    gp.wait_ge(idx_done, 2)
                gp.tensor_copy(idx_b[:, 0, :], idx_b0[:, :]).then_inc(idx_next, 1)
                gp.wait_ge(idx_next, BLOCKS * half + 1)
                if half:
                    gp.wait_ge(up_mm, half * STEPS)
                else:
                    gp.wait_ge(b_first_out, 2 * 16)
                gather_b(half, 0, 0, 0, first=True)
                if half == 0:
                    split_odd(1)
                gather_b(half, 1, 0, 1, first=True)
                if half:
                    clear_v(TILES - 1)
                else:
                    gather_tile(3)

            def early_steps(half):
                for t in range(EARLY):
                    if half == 0 and t + 2 < TILES:
                        split_odd(t + 2)
                    step_lo(t % 2, half * STEPS + t)
                    gp.wait_ge(up_mm, half * STEPS + t + 1)
                    m = t + 2
                    if m == TILES:
                        for j in range(BCH):
                            gp.wait_ge(b_out[j], 2 * 16)
                        next_block(1, BLOCKS * half + 2)
                    gather_b(half, m, m // TILES, m % 2, first=m < TILES)
                    if half == 0 and t == 0:
                        gather_tile(4)
                    if half == 0 and t < 2:
                        pair_work(0, t)

            def clear_v(t):
                gp.wait_ge(v_done, t + 1)
                gp.memset(vacc[:, t * TOK:(t + 1) * TOK], 0.0).then_inc(v_zero, 1)

            def pair_work(i, k):
                c, slot = k % TILES, k // TILES
                q = i * 2 + (HPAIRS + slot)
                e = comb(q)
                if c == 0:
                    src = (idx_w[:, q, :] if isinstance(q, int)
                           else idx_w[:, bass.ds(q, 1), :].rearrange("p a b -> p (a b)"))
                    gp.tensor_copy(idx_now[:, :], src).then_inc(pool_step, 1)
                    if not (isinstance(q, int) and q == HPAIRS):
                        gp.wait_ge(e_sum_done, e)
                    wait_before_gather(pool_step, i * 2 + (chain[0] + slot + 1))
                    gather_rows(ea_one[:, 0, :], w0_rows, idx_now[:, 0:1], e_in)
                    gather_rows(eb_one[:, 0, :], e_table, idx_now[:, 1:2], e_in)
                elif c == 1:
                    comb_in(e)
                elif c == 2:
                    split_x(q, 0, xn[:, slot, :], False)
                    comb_out(e)

            def body(half, i, last, start=0):
                for k in range(start, BODY):
                    n = i * BODY + (half * STEPS + k)
                    if not (last and k == BODY - 1):
                        step_lo((k + 1) % 2, n + 1)
                    if not (last and k + 3 >= BODY):
                        m = k + 3
                        if m % TILES == 0:
                            next_block((m // TILES) % 2, i * 2 + (BLOCKS * half + m // TILES + 1))
                        wait_before_gather(up_mm, n + 2)
                        gather_b(half, m, (m // TILES) % 2, m % 2)
                    if last and k == BODY - 1:
                        for to_half, to_blk, ch, to_slot in next_half(half, TILES - 2):
                            if to_blk == ADAPTERS_IN:
                                w_low(to_half, to_blk, ch, to_slot)
                    if half == 0:
                        pair_work(i, k)
                        if last and k > TILES:
                            clear_v(k - TILES - 1)

            gather_tile(1)
            split_odd(0)
            gather_tile(2)
            for half in range(HALVES):
                half_start(half)
                early_steps(half)
                body(half, 0, False, start=EARLY - 1)
                with gp.Fori(1, TURNS - 1) as i:
                    body(half, i, False)
                body(half, TURNS - 1, True)

        @block.scalar
        def _(act):
            def copy(dst, src):
                return act.activation(dst, src, ACT.Copy)

            def comb_in(e, n):
                act.wait_ge(e_t_done, e + 1)
                if not (isinstance(e, int) and e == 0):
                    act.wait_ge(e_mm, e)
                copy(et_hi[:, 0:n, :], (em_four if n == TP else em_one)[:, 0:n, :])
                copy(eb_hi[:, 0:n, :], eb_four[e] if n == TP else eb_one[:, :, :]).then_inc(e_hi_done, 1)

            def comb_out(e, n, layers):
                act.wait_ge(e_masked, e)
                if not (isinstance(layers, int) and layers == 0):
                    act.wait_ge(layer_mm, layers)
                em = em_four if n == TP else em_one
                copy(bd_hi[:, 0:n, :], em[:, 0:n, :]).then_inc(bd_hi_done, 1)

            def split_x(q, j, source, first_half):
                hi, _ = layer_in(j, first_half)
                copy(hi, source).then_inc(lx_hi, 1)

            def w_high(half, blk, c, slot):
                lo, hi = CHUNKS[c]
                act.wait_ge(raw_in[c], raw_loads(half, blk, c) * 16)
                copy(w_hi[:, slot, lo:hi], w_raw[:, lo:hi]).then_inc(w_hi_done, 1)

            def transpose(half, t):
                g = half * TILES + t
                if g == 1:
                    for j in range(2, BCH):
                        act.wait_ge(b_out[j], 2 * 16)
                for c, psum in enumerate(tile_banks(t)[0]):
                    act.wait_ge(tr_mm, g * KC + c + 1)
                    copy(xt_hi[:, c, t * TOK:(t + 1) * TOK], psum[:, :]).then_inc(xt_hi_done, 1)

            def products(half, t):
                g = half * TILES + t
                for m, psum in enumerate(tile_banks(t)[1]):
                    act.wait_ge(a_mm, g * 2 + m + 1)
                    if g:
                        act.wait_ge(sel_mm, g * TP)
                    if half:
                        act.wait_ge(layer_mm, PAIRS)
                    copy(ua_parts[m][0], psum[:, :]).then_inc(ua_hi, 1)

            def opening(events):
                for what, m in events:
                    if what == "comb_in":
                        comb_in(m, TP)
                    elif what == "comb_out" and m:
                        comb_out(m, TP, (m - 1) * TP)
                    elif what == "b":
                        act.wait_ge(b_in[m], 16)
                        copy(b_parts[m][0], b_raws[m]).then_inc(b_hi_done, 1)
                    elif what == "x":
                        act.wait_ge(x_in[m], 16)
                        if m:
                            act.wait_ge(layer_mm, m * TP)
                        for j in range(TP):
                            split_x(m * TP + j, j, acc[:, m * TP + j, :], True)
                    elif what == "w":
                        for c in range(ACH if m == ADAPTERS_IN else NCH):
                            w_high(0, m, c, 1 if m == ADAPTERS_IN else 0)
                    elif what == "transpose":
                        transpose(0, m)
                    elif what == "products":
                        products(0, m)

            def step_silu(n, slot):
                act.wait_ge(gate_mm, n + 1)
                act.wait_ge(h_done, hs(n))
                act.activation(silu[:, :], pg[slot][:, :], ACT.Silu).then_inc(silu_done, 1)

            def step_hi(n, slot, first=False):
                act.wait_ge(h_done, hs(n + 1))
                if not first:
                    act.wait_ge(down_mm, downs((n - 1) * DB))
                copy(h_hi[:, slot, :], h[:, :]).then_inc(h_hi_done, 1)

            def v_high(half, t):
                cols = slice(t * TOK, (t + 1) * TOK)
                act.wait_ge(v_masked, half * TILES + t + 1)
                act.wait_ge(up_mm, (half + 1) * STEPS - TILES + t + 1)
                copy(u[:, 0, cols], vacc[:, cols]).then_inc(v_hi_done, 1)

            def pair_work(i, k):
                c, slot = k % TILES, k // TILES
                q = i * 2 + (HPAIRS + slot)
                e = comb(q)
                if c == 1:
                    comb_in(e, 1)
                elif c == 2:
                    if isinstance(q, int) and q == HPAIRS:
                        act.wait_ge(sel_mm, TILES * TP)
                    act.wait_ge(layer_mm, q)
                    act.wait_ge(xn_in[slot], i * 16 + 16)
                    split_x(q, 0, xn[:, slot, :], False)
                    comb_out(e, 1, q)

            def first_block(half, k):
                for c in FIRST_BLOCK[k]:
                    act.wait_ge(a_mm, 2 * TILES * (half + 1))
                    if half and c >= ACH:
                        act.wait_ge(down_mm, downs(half * STEPS * DB))
                    w_high(half, 1, c, 1)

            def early_steps(half):
                for t in range(EARLY):
                    step_silu(half * STEPS + t, t % 2)
                    if half == 0 and t + 2 < TILES:
                        opening((("x", t + 2),))
                    transpose(half, t + 1)
                    step_hi(half * STEPS + t, t % 2, first=half * STEPS + t == 0)
                    if half == 0 and t + 3 <= TILES:
                        comb_in(t + 3, TP)
                    products(half, t + 1)
                    if half == 0 and t + 3 <= TILES:
                        comb_out(t + 3, TP, (t + 2) * TP)
                    first_block(half, t)
                    if half == 0 and t < 2:
                        pair_work(0, t)

            def body(half, i, last, start=0):
                first = isinstance(i, int) and i == 0
                for k in range(start, BODY):
                    n = i * BODY + (half * STEPS + k)
                    c, slot = k % TILES, k // TILES
                    blk = i * 2 + slot
                    if last and k > TILES:
                        v_high(half, k - TILES - 1)
                    if not (last and k == BODY - 1):
                        step_silu(n + 1, (k + 1) % 2)
                        step_hi(n + 1, (k + 1) % 2)
                    if first and slot == 0:
                        if k >= EARLY:
                            first_block(half, k)
                    elif last and slot == 1:
                        for to_half, to_blk, ch, to_slot in next_half(half, c):
                            if to_blk == ADAPTERS_IN:
                                act.wait_ge(up_mm, to_half * STEPS)
                            else:
                                act.wait_ge(down_mm, downs((n - c) * DB))
                            w_high(to_half, to_blk, ch, to_slot)
                    else:
                        act.wait_ge(down_mm, downs((n - c) * DB))
                        w_high(half, blk + 1, c, 1 - slot)
                    if half == 0:
                        pair_work(i, k)

            opening(OPENING)
            act.wait_ge(bdn_in, 16)
            copy(bdn_hi[:, :], silu[:, :]).then_inc(bdn_hi_done, 1)
            act.wait_ge(bdn_done, 1)
            act.sem_inc(silu_done, 1)
            for half in range(HALVES):
                if half:
                    transpose(half, 0)
                    v_high(half - 1, TILES - 1)
                    products(half, 0)
                early_steps(half)
                body(half, 0, False, start=EARLY - 1)
                with act.Fori(1, TURNS - 1) as i:
                    body(half, i, False)
                body(half, TURNS - 1, True)
            v_high(HALVES - 1, TILES - 1)

        @block.vector
        def _(dve):
            chain = [0]

            def link(ins):
                chain[0] += 1
                ins.then_inc(dve_step, 1)
                dve.wait_ge(dve_step, chain[0])

            def masked(dst, src, n):
                return dve.tensor_tensor(
                    dst[:, 0:n, :].rearrange("p j (s d) -> p j s d", s=2),
                    src.unsqueeze(2).to_broadcast([P, n, 2, C]),
                    half_mask[:, :].unsqueeze(1).unsqueeze(3).to_broadcast([P, n, 2, C]), ALU.mult)

            def comb_in(e):
                if e == 0:
                    dve.wait_ge(e0_in, 2 * 16)
                else:
                    dve.wait_ge(e_tile_in[e - 1], 2 * TP * 16)
                if e >= 2:
                    dve.wait_ge(bd_done, e - 1)
                elif e == 1:
                    dve.wait_ge(e_lo_done, 1)
                masked(em_four, ea_four[e][:, :, C:2 * C], TP).then_inc(e_t_done, 1)
                if e == 1:
                    dve.wait_ge(e_out, 16)
                elif e >= 2:
                    dve.wait_ge(e_masked, e - 1)
                dve.tensor_tensor(e_sum[:, :, :], ea_four[e][:, :, 0:C], eb_four[e], ALU.add
                                  ).then_inc(e_sum_done, 1)
                if e == 0:
                    gather_numbers()
                dve.wait_ge(e_hi_done, e + 1)
                dve.tensor_tensor(et_lo[:, :, :], em_four, et_hi[:, :, :], ALU.subtract)
                dve.tensor_tensor(eb_lo[:, :, :], eb_four[e], eb_hi[:, :, :], ALU.subtract
                                  ).then_inc(e_lo_done, 1)

            def comb_in_one(e):
                dve.wait_ge(e_in, (e - TILES) * 2 * 16)
                dve.wait_ge(bd_done, e - 1)
                masked(em_one, ea_one[:, :, C:2 * C], 1).then_inc(e_t_done, 1)

            def comb_out(e, n, meanwhile=None):
                dve.wait_ge(e_mm, e + 1)
                dve.wait_ge(e_sum_done, e + 1)
                product = combination_bank(e)[:, 0:n * C].rearrange("p (j d) -> p j d", j=n)
                dve.tensor_tensor(e_sum[:, 0:n, :], product, e_sum[:, 0:n, :], ALU.add).then_inc(e_add, 1)
                if not (isinstance(e, int) and e == 0):
                    dve.wait_ge(e_add, e + 1)
                    masked(em_four if n == TP else em_one, e_sum[:, 0:n, :], n).then_inc(e_masked, 1)
                if meanwhile:
                    meanwhile()
                if isinstance(e, int) and 0 < e <= TILES:
                    dve.wait_ge(bd_hi_done, e)
                    dve.tensor_tensor(bd_lo[:, :, :], em_four, bd_hi[:, :, :], ALU.subtract
                                      ).then_inc(bd_done, 1)

            def w_low(half, blk, c, slot):
                lo, hi = CHUNKS[c]
                dve.wait_ge(w_hi_done, conv(half, blk, c))
                dve.tensor_tensor(w_lo[:, slot, lo:hi], w_raw[:, lo:hi], w_hi[:, slot, lo:hi],
                                  ALU.subtract).then_inc(w_done, 1)

            def add_layer(q, dst, psum, bias_col):
                dve.wait_ge(layer_mm, q + 1)
                dve.scalar_tensor_tensor(out=dst, in0=psum[:, :], scalar=bias_col, in1=dst,
                                         op0=ALU.add, op1=ALU.add).then_inc(layer_add, 1)

            def transpose(half, t):
                g = half * TILES + t
                cols = slice(t * TOK, (t + 1) * TOK)
                for c, psum in enumerate(tile_banks(t)[0]):
                    dve.wait_ge(xt_hi_done, g * KC + c + 1)
                    dve.tensor_tensor(xt_lo[:, c, cols], psum[:, :], xt_hi[:, c, cols], ALU.subtract
                                      ).then_inc(xt_done, 1)

            def products(half, t):
                g = half * TILES + t
                for m, psum in enumerate(tile_banks(t)[1]):
                    dve.wait_ge(ua_hi, g * 2 + m + 1)
                    dve.tensor_tensor(ua_parts[m][1], psum[:, :], ua_parts[m][0], ALU.subtract
                                      ).then_inc(ua_done, 1)

            def selectors(half, t, pairs):
                g = half * TILES + t
                for j in pairs:
                    first = 2 * (half * HPAIRS + t * TP + j)
                    if g * TP + j >= 2:
                        dve.wait_ge(sel_mm, g * TP + j - 1)
                    dve.tensor_tensor(
                        sel[:, j % 2],
                        pattern[:, :, :].unsqueeze(2).to_broadcast([P, 2, 2, 4 * RANK]),
                        onehot[:, first:first + 2].unsqueeze(1).unsqueeze(3).to_broadcast([P, 2, 2, 4 * RANK]),
                        ALU.mult).then_inc(sel_done, 1)

            def select(half, t):
                g = half * TILES + t
                if g == 0:
                    for j in range(2):
                        dve.wait_ge(b_out[j], 2 * 16)
                if half:
                    dve.wait_ge(bdown_mm, (half - 1) * HPAIRS + TP * (t + 1))
                dve.wait_ge(sel_mm, (g + 1) * TP)
                for m, psum in enumerate(tile_banks(t)[2]):
                    dve.tensor_tensor(
                        u[:, m, t * TOK:(t + 1) * TOK].rearrange("p (j s c) -> p j s c", j=TP, s=2),
                        psum[:, :].rearrange("p (j s c) -> p j s c", j=TP, s=2),
                        half_mask[:, :].unsqueeze(1).unsqueeze(3).to_broadcast([P, TP, 2, C]),
                        ALU.mult).then_inc(u_done, 1)

            def opening(events):
                for what, m in events:
                    if what == "comb_in":
                        comb_in(m)
                    elif what == "comb_out":
                        comb_out(m, TP, (lambda: selectors(0, 0, (2, 3))) if m == 2 else None)
                    elif what == "b":
                        dve.wait_ge(b_hi_done, m + 1)
                        dve.tensor_tensor(b_parts[m][1], b_raws[m], b_parts[m][0], ALU.subtract
                                          ).then_inc(b_lo_done, 1)
                    elif what == "x":
                        for j in (0, 2):
                            q = m * TP + j
                            hi, lo = layer_in(j, True)
                            dve.wait_ge(lx_hi, q + 1)
                            dve.tensor_tensor(lo, acc[:, q, :], hi, ALU.subtract).then_inc(lx_lo_v, 1)
                    elif what == "layer":
                        for j in range(TP):
                            q = m * TP + j
                            if q % 2:
                                dve.wait_ge(lx_lo_p, lows(q))
                            add_layer(q, acc[:, q, :], layer_bank[j], bias[:, q:q + 1])
                    elif what == "w":
                        for c in range(ACH if m == ADAPTERS_IN else NCH):
                            w_low(0, m, c, 1 if m == ADAPTERS_IN else 0)
                    elif what == "transpose":
                        transpose(0, m)
                    elif what == "products":
                        selectors(0, m, (0, 1))
                        products(0, m)
                    elif what == "select":
                        select(0, m)

            dve.wait_ge(consts, 2)
            p0 = p_int[:, 0:1]
            link(dve.tensor_scalar(p_int[:, 5:6], p0, 6, None, ALU.logical_shift_right))
            link(dve.tensor_copy(half_mask[:, 1:2], p_int[:, 5:6]))
            link(dve.tensor_scalar(half_mask[:, 0:1], half_mask[:, 1:2], -1.0, 1.0, ALU.mult, ALU.add))

            def gather_numbers():
                link(dve.tensor_scalar(p_int[:, 2:3], p0, 63, None, ALU.bitwise_and))
                dve.tensor_copy(p_f[:, 1:2], p_int[:, 2:3])
                dve.wait_ge(ints_in, 4 * 16)
                for s in range(2):
                    rows = slice(s * C, (s + 1) * C)
                    by_pair = ints[rows, :, :].rearrange("p k (q s) -> p k q s", s=2)
                    dve.tensor_copy(pair_su[rows, :], by_pair[:, 0, :, s])
                    ins = dve.tensor_copy(pair_ad[rows, :], by_pair[:, 1, :, s])
                link(ins)
                dve.tensor_scalar(idx_w[:, :, 0], pair_su[:, :], float(C), p_f[:, 1:2], ALU.mult, ALU.add)
                dve.tensor_scalar(idx_w[:, :, 1], pair_ad[:, :], float(C), p_f[:, 1:2], ALU.mult, ALU.add
                                  ).then_inc(idx_done, 1)

            def block_numbers():
                dve.tensor_scalar(p_int[:, 1:2], p0, 4, None, ALU.logical_shift_right)
                dve.tensor_scalar(p_int[:, 3:4], p0, 5, 1, ALU.logical_shift_right, ALU.bitwise_and)
                dve.tensor_scalar(r_int2[:, :], r_int[:, :], 15, None, ALU.bitwise_and)
                dve.tensor_copy(adf[:, :], ints[:, 1, :])
                link(dve.tensor_scalar(p_int[:, 4:5], p0, 15, None, ALU.bitwise_and))
                dve.tensor_copy(p_f[:, 0:1], p_int[:, 1:2])
                link(dve.tensor_scalar(p_f[:, 2:3], p_int[:, 3:4], float(P), None, ALU.mult))
                link(dve.tensor_tensor(p_f[:, 3:4], p_f[:, 2:3], p_int[:, 4:5], ALU.add))
                link(dve.tensor_scalar(p_f[:, 2:3], p_f[:, 3:4], float(BLOCKS), None, ALU.mult))
                dve.tensor_scalar(idx_f[:, :], pair_ad[:, :], float(RANK), p_f[:, 3:4], ALU.mult, ALU.add)
                dve.tensor_scalar(idx_b0[:, :], pair_ad[:, :], float(RANK * BLOCKS), p_f[:, 2:3],
                                  ALU.mult, ALU.add).then_inc(idx_done, 1)

            def tables():
                link(dve.memset(pattern[:, :, :], 0.0))
                for part in range(2):
                    for term in (part, part + 2):
                        dve.tensor_scalar(pattern[:, part, term * RANK:(term + 1) * RANK], r_int2[:, :],
                                          0.0, None, ALU.is_equal)
                link(dve.tensor_scalar(onehot[:, :], adf[:, :], p_f[:, 0:1], None, ALU.is_equal))
                for a in range(ADAPTERS):
                    link(dve.tensor_scalar((bias_n if a else bias)[:, :], pair_ad[:, :], float(a),
                                           bias_src[:, a:a + 1], ALU.is_equal, ALU.mult))
                    if a:
                        link(dve.tensor_tensor(bias[:, :], bias[:, :], bias_n[:, :], ALU.add))

            def step_h(n, slot, first=False):
                dve.wait_ge(up_mm, n + 1)
                dve.wait_ge(silu_done, silus(n + 1))
                if not first:
                    dve.wait_ge(h_lo_done, n)
                dve.tensor_tensor(h[:, :], silu[:, :], pu[slot][:, :], ALU.mult).then_inc(h_done, 1)

            def v_low(half, t):
                cols = slice(t * TOK, (t + 1) * TOK)
                dve.wait_ge(v_hi_done, half * TILES + t + 1)
                dve.tensor_tensor(u[:, 1, cols], vacc[:, cols], u[:, 0, cols], ALU.subtract).then_inc(v_done, 1)

            def v_mask(half, t):
                cols = slice(t * TOK, (t + 1) * TOK)
                first = 2 * (half * HPAIRS + t * TP)
                dve.wait_ge(down_add, adds(((half + 1) * STEPS - TILES + t + 1) * DB))
                v3 = vacc[:, cols].rearrange("p (s c) -> p s c", c=C)
                dve.tensor_tensor(
                    v3, v3, onehot[:, first:first + 2 * TP].unsqueeze(2).to_broadcast([P, 2 * TP, C]),
                    ALU.mult).then_inc(v_masked, 1)

            def finish(half, t, banks=finish_banks, pairs=range(TP)):
                for j in pairs:
                    q = t * TP + j
                    dve.wait_ge(bdown_mm, half * HPAIRS + q + 1)
                    dve.tensor_tensor(acc[:, q, :], banks[j][:, :], acc[:, q, :], ALU.add).then_inc(y_add, 1)

            def add_down(n, t, results=range(DB)):
                for b in results:
                    dve.wait_ge(down_mm, downs(n * DB + (b + 1)))
                    if b == 2:
                        dst, psum = vacc[:, t * TOK:(t + 1) * TOK], pv
                    else:
                        j = b if b < 2 else b - 1
                        dst, psum = acc[:, t * TP + j, :], pd[j % 2]
                    dve.tensor_tensor(dst, psum[:, :], dst, ALU.add).then_inc(down_add, 1)

            def pair_work(i, k):
                c, slot = k % TILES, k // TILES
                q = i * 2 + (HPAIRS + slot)
                e = comb(q)
                if c == 1:
                    comb_in_one(e)
                elif c == 2:
                    comb_out(e, 1)
                elif c == 3:
                    dve.wait_ge(lx_lo_p, lows(q))
                    add_layer(q, xn[:, slot, :], px,
                              bias[:, q:q + 1] if isinstance(q, int) else bias[:, bass.ds(q, 1)])

            def early_steps(half):
                for t in range(EARLY):
                    if half == 0:
                        opening((("layer", t + 1),))
                        if t + 2 < TILES:
                            opening((("x", t + 2),))
                    transpose(half, t + 1)
                    step_h(half * STEPS + t, t % 2, first=half * STEPS + t == 0)
                    if half == 0 and t + 3 <= TILES:
                        comb_in(t + 3)
                    selectors(half, t + 1, (0, 1))
                    products(half, t + 1)
                    if t == 0:
                        dve.wait_ge(v_zero, 1 + half * TILES)
                    add_down(half * STEPS + t, t, range(DB - 1))
                    selectors(half, t + 1, (2, 3))
                    add_down(half * STEPS + t, t, (DB - 1,))
                    select(half, t + 1)
                    if half == 0 and t + 3 <= TILES:
                        comb_out(t + 3, TP)
                    for c in FIRST_BLOCK[t]:
                        w_low(half, 1, c, 1)
                    if half == 0 and t < 2:
                        pair_work(0, t)

            def body(half, i, last, start=0):
                first = isinstance(i, int) and i == 0
                for k in range(start, BODY):
                    n = i * BODY + (half * STEPS + k)
                    c, slot = k % TILES, k // TILES
                    blk = i * 2 + slot
                    if last and TILES < k < BODY - 1:
                        v_low(half, k - TILES - 1)
                        finish(half, k - TILES - 1)
                    if not (last and k == BODY - 1):
                        step_h(n + 1, (k + 1) % 2)
                    if last and k == BODY - 1:
                        add_down(n, c, range(DB - 2))
                        v_low(half, c - 1)
                        add_down(n, c, range(DB - 2, DB))
                    elif k >= start + (1 if start else 0):
                        add_down(n, c)
                    if last and slot == 1:
                        v_mask(half, c)
                    if first and slot == 0:
                        if k >= EARLY:
                            for ch in FIRST_BLOCK[k]:
                                w_low(half, 1, ch, 1)
                    elif last and slot == 1:
                        for to_half, to_blk, ch, to_slot in next_half(half, c):
                            if to_blk != ADAPTERS_IN:
                                w_low(to_half, to_blk, ch, to_slot)
                    else:
                        w_low(half, blk + 1, c, 1 - slot)
                    if half == 0:
                        pair_work(i, k)

            opening(OPENING[:1])
            block_numbers()
            opening(OPENING[1:2])
            tables()
            opening(OPENING[2:])
            dve.wait_ge(bdn_hi_done, 1)
            dve.tensor_tensor(bdn_lo[:, :], silu[:, :], bdn_hi[:, :], ALU.subtract).then_inc(bdn_done, 1)
            dve.wait_ge(b_lo_done, BCH)
            dve.memset(vacc[:, :], 0.0).then_inc(v_zero, 1)
            dve.sem_inc(h_done, 1)
            dve.sem_inc(down_add, 1)
            for half in range(HALVES):
                if half:
                    transpose(half, 0)
                    finish(half - 1, TILES - 2, last_banks)
                    v_low(half - 1, TILES - 1)
                    selectors(half, 0, (0, 1))
                    products(half, 0)
                    finish(half - 1, TILES - 1, last_banks)
                    selectors(half, 0, (2, 3))
                    select(half, 0)
                early_steps(half)
                body(half, 0, False, start=EARLY - 1)
                with dve.Fori(1, TURNS - 1) as i:
                    body(half, i, False)
                body(half, TURNS - 1, True)
            finish(HALVES - 1, TILES - 2, last_banks, range(1))
            v_low(HALVES - 1, TILES - 1)
            finish(HALVES - 1, TILES - 2, last_banks, range(1, TP))
            finish(HALVES - 1, TILES - 1, last_banks)

        @block.tensor
        def _(pe):
            def split_product(psum, w_parts, x_parts, chunks=1, close=True, fresh=True):
                done = 0
                for c in range(chunks):
                    for wi, xi in ((0, 0), (0, 1), (1, 0)):
                        ins = pe.matmul(psum, w_parts[wi](c), x_parts[xi](c), start=(fresh and done == 0),
                                        stop=(close and done == 3 * chunks - 1))
                        done += 1
                return ins

            def combine(e, n):
                pe.wait_ge(e_lo_done, e + 1)
                for j in range(n):
                    ins = split_product(combination_bank(e)[:, j * C:(j + 1) * C],
                                        [lambda c, w=w: w[:, j, :] for w in (et_hi, et_lo)],
                                        [lambda c, w=w: w[:, j, :] for w in (eb_hi, eb_lo)])
                ins.then_inc(e_mm, 1)

            def layer(q, j, psum, first_half):
                hi, lo = layer_in(j, first_half)
                pe.wait_ge(lx_lo_v if first_half and q % 2 == 0 else lx_lo_p, lows(q))
                split_product(psum[:, :], [lambda c: bd_hi[:, j, :], lambda c: bd_lo[:, j, :]],
                              [lambda c: hi, lambda c: lo]).then_inc(layer_mm, 1)

            def layers(t):
                pe.wait_ge(bd_done, t + 1)
                for j in range(TP):
                    layer(t * TP + j, j, layer_bank[j], True)

            def transpose(half, t):
                g = half * TILES + t
                if half == 0:
                    pe.wait_ge(layer_add, (t + 1) * TP)
                else:
                    pe.wait_ge(x3_in[t], 16)
                for c, psum in enumerate(tile_banks(t)[0]):
                    for j in range(TP):
                        ins = pe.transpose(psum[:, j * P:(j + 1) * P],
                                           acc[:, t * TP + j, c * P:(c + 1) * P], ident[:, :])
                    ins.then_inc(tr_mm, 1)

            def products(half, t):
                g = half * TILES + t
                cols = slice(t * TOK, (t + 1) * TOK)
                pe.wait_ge(w_done, conv(half, ADAPTERS_IN, ACH - 1))
                for m, psum in enumerate(tile_banks(t)[1]):
                    for c in range(KC):
                        if m == 0:
                            pe.wait_ge(xt_done, g * KC + c + 1)
                        ins = split_product(psum[:, :],
                                            [lambda _, w=w: w[:, 1, (m * KC + c) * P:(m * KC + c + 1) * P]
                                             for w in (w_hi, w_lo)],
                                            [lambda _, s=s: s[:, c, cols] for s in (xt_hi, xt_lo)],
                                            fresh=c == 0, close=c == KC - 1)
                    ins.then_inc(a_mm, 1)

            def select(half, t, pairs=range(TP)):
                g = half * TILES + t
                pe.wait_ge(ua_done, (g + 1) * 2)
                for j in pairs:
                    pe.wait_ge(sel_done, g * TP + j + 1)
                    for m, psum in enumerate(tile_banks(t)[2]):
                        for part in range(2):
                            ins = pe.matmul(psum[:, j * P:(j + 1) * P],
                                            sel[:, j % 2, part].rearrange("p s e -> p (s e)"),
                                            ua_parts[m][part][:, j * P:(j + 1) * P],
                                            start=(part == 0), stop=(part == 1))
                    ins.then_inc(sel_mm, 1)

            def hidden(half, m, n, t, wslot, slot, blk, loads, selections=0, between=None):
                psum, base, done = ((pg[slot], GATE, gate_mm), (pu[slot], UP, up_mm))[m]
                cols = slice(t * TOK, (t + 1) * TOK)
                pe.wait_ge(w_done, conv(half, blk, m))
                if not (isinstance(n, int) and n % STEPS == 0):
                    pe.wait_ge(*((silu_done, silus(n - 1)), (h_done, hs(n - 1)))[m])
                split_product(psum[:, :],
                              [lambda c, w=w: w[:, wslot, base + c * P:base + (c + 1) * P] for w in (w_hi, w_lo)],
                              [lambda c, s=s: s[:, c, cols] for s in (xt_hi, xt_lo)],
                              chunks=KC, close=False)
                if between:
                    between()
                if m == 0:
                    pe.wait_ge(b_got_in[slot], loads)
                if selections:
                    pe.wait_ge(u_done, selections)
                for j in range(TP):
                    ins = pe.matmul(psum[:, j * P:(j + 1) * P], b_got[:, slot, j, m * P:(m + 1) * P],
                                    u[:, m, t * TOK + j * P:t * TOK + (j + 1) * P],
                                    start=False, stop=(j == TP - 1))
                ins.then_inc(done, 1)

            def down(half, n, wslot, slot, blk, next_tile=None):
                pe.wait_ge(h_lo_done, n + 1)
                pe.wait_ge(w_done, conv(half, blk, NCH - 1))
                for b in range(DB):
                    if b == 0:
                        pe.wait_ge(down_add, adds(n * DB))
                    elif b > 2:
                        pe.wait_ge(down_add, adds(n * DB + (b - 2)))
                    if next_tile is not None and b == 2:
                        pe.wait_ge(ua_done, (half * TILES + next_tile) * 2 + 1)
                    if next_tile is not None and b == DB - 1:
                        select(half, next_tile, range(TP - 2))
                    if b == 2:
                        ins = split_product(pv[:, :],
                                            [lambda c, w=w: w[:, wslot, ADOWN:ADOWN + P] for w in (w_hi, w_lo)],
                                            [lambda c, s=s: s[:, slot, :] for s in (h_hi, h_lo)])
                    else:
                        j = b if b < 2 else b - 1
                        ins = split_product(pd[j % 2][:, :],
                                            [lambda c, s=s: s[:, slot, j * P:(j + 1) * P] for s in (h_hi, h_lo)],
                                            [lambda c, w=w: w[:, wslot, DOWN:DOWN + T] for w in (w_hi, w_lo)])
                    ins.then_inc(down_mm, 1)
                if next_tile is not None:
                    select(half, next_tile, range(TP - 2, TP))

            def finish(half, t, banks=finish_banks):
                pe.wait_ge(v_done, half * TILES + t + 1)
                for j in range(TP):
                    q = t * TP + j
                    if banks is finish_banks and j == TP - 1:
                        pe.wait_ge(y_add, half * HPAIRS + t * TP + 1)
                    elif banks is last_banks and t == TILES - 1:
                        pe.wait_ge(y_add, half * HPAIRS + q - TP + 1)
                    elif banks is last_banks and j:
                        pe.wait_ge(down_add, adds((half + 1) * STEPS * DB - DB + j + 2))
                    split_product(banks[j][:, :],
                                  [lambda c, m=m: u[:, m, q * P:(q + 1) * P] for m in range(2)],
                                  [lambda c, w=w: w[:, :] for w in (bdn_hi, bdn_lo)]
                                  ).then_inc(bdown_mm, 1)

            def warm_up(products):
                for _ in range(products):
                    pe.matmul(pg[0][:, 0:P], ident[:, :], ident[:, :], start=True, stop=True)

            def opening(events):
                for what, m in events:
                    if what == "comb_out":
                        if m == 0:
                            warm_up(WARM_UP[0])
                        elif m == 1:
                            pe.wait_ge(w_done, conv(0, 0, NCH - 1))
                            warm_up(WARM_UP[1])
                        if m:
                            pe.wait_ge(e_add, m)
                        if m == 2:
                            pe.wait_ge(layer_add, TP)
                        combine(m, TP)
                    elif what == "layer":
                        warm_up(WARM_UP[2])
                        layers(m)
                    elif what == "transpose":
                        transpose(0, m)
                    elif what == "products":
                        products(0, m)
                    elif what == "select":
                        select(0, m)

            def early_steps(half):
                g0, n0 = half * TILES, half * STEPS
                for t in range(EARLY):
                    n = n0 + t
                    step = (half, n, t, 0, t % 2, 0, (n // 2 + 1) * TP * 16, (g0 + t + 1) * 2)
                    hidden(step[0], 0, *step[1:])
                    if t:
                        pe.wait_ge(down_add, adds(n * DB))
                    if half == 0:
                        if t == 0:
                            pe.wait_ge(layer_add, TP)
                        pe.wait_ge(e_add, t + 3)
                        layers(t + 1)
                    hidden(step[0], 1, *step[1:], between=lambda: transpose(half, t + 1))
                    products(half, t + 1)
                    down(half, n, 0, t % 2, 0, next_tile=t + 1)
                    if half == 0 and t + 3 <= TILES:
                        pe.wait_ge(down_add, adds(n * DB + 4))
                        combine(t + 3, TP)

            def pair_work(i, k):
                c, slot = k % TILES, k // TILES
                q = i * 2 + (HPAIRS + slot)
                if c == 2:
                    pe.wait_ge(layer_add, q)
                    combine(comb(q), 1)
                elif c == 3:
                    pe.wait_ge(e_add, comb(q) + 1)
                    pe.wait_ge(bd_done, comb(q))
                    layer(q, 0, px, False)

            def body(half, i, last, start=0):
                for k in range(start, BODY):
                    n = i * BODY + (half * STEPS + k)
                    slot = k // TILES
                    m = k + 1
                    nxt = (half, n + 1, m % TILES, (m // TILES) % 2, m % 2, i * 2 + m // TILES,
                           i * (BODY * TP * 8) + ((half * STEPS + m) // 2 + 1) * TP * 16,
                           (half * TILES + TILES) * 2 if start and k == start else 0)
                    if not (last and k == BODY - 1):
                        hidden(nxt[0], 0, *nxt[1:])
                    if last and TILES < k < BODY - 1:
                        pe.wait_ge(down_add, adds(n * DB))
                        finish(half, k - TILES - 1)
                    if not (last and k == BODY - 1):
                        hidden(nxt[0], 1, *nxt[1:])
                    if last and TILES < k < BODY - 1:
                        pe.wait_ge(y_add, half * HPAIRS + TP * (k - TILES))
                    if not (start and k == start):
                        down(half, n, slot, k % 2, i * 2 + slot)
                    if half == 0:
                        pair_work(i, k)

            pe.wait_ge(consts, 3)
            pe.sem_inc(down_mm, 1)
            opening(OPENING)
            for half in range(HALVES):
                if half:
                    pe.wait_ge(silu_done, silus(half * STEPS))
                    pe.wait_ge(h_done, hs(half * STEPS))
                    transpose(half, 0)
                    pe.wait_ge(layer_add, PAIRS)
                    finish(half - 1, TILES - 2, last_banks)
                    products(half, 0)
                    finish(half - 1, TILES - 1, last_banks)
                    select(half, 0)
                    pe.wait_ge(y_add, half * HPAIRS)
                early_steps(half)
                body(half, 0, False, start=EARLY - 1)
                with pe.Fori(1, TURNS - 1) as i:
                    body(half, i, False)
                body(half, TURNS - 1, True)
            for t in (TILES - 2, TILES - 1):
                finish(HALVES - 1, t, last_banks)


def kernel(x, itok_B_1_198, itok_B_0_7, fside_8xS_0, L0_cond_weights, L1_cond_weights, L2_cond_weights,
           L3_cond_Wg, L3_cond_Wu, L3_cond_Wd, L3_cond_Ag, L3_cond_Bg, L3_cond_Au, L3_cond_Bu,
           L3_cond_Ad, L3_cond_Bd):
    import numpy as np
    import concourse.bacc as bacc
    from concourse.bass_utils import run_bass_kernel_spmd

    def a(v):
        return np.asarray(v)

    def by_block(w):
        return a(w).reshape(KC, P, BLOCKS, P).transpose(2, 1, 0, 3).reshape(BLOCKS, P, KC * P)

    def adapters_in(w):
        return a(w).reshape(ADAPTERS, KC, P, RANK).transpose(2, 1, 0, 3).reshape(P, KC * P)

    def adapters_out(w):
        return a(w).reshape(P, BLOCKS, 1, P)

    def with_transposed(w):
        return np.concatenate([a(w), a(w).transpose(0, 2, 1)], axis=2).reshape(-1, 2 * C)

    arrays = {
        "x": a(x),
        "subject": a(itok_B_1_198),
        "adapter": a(itok_B_0_7),
        "w0_rows": with_transposed(L0_cond_weights),
        "w1_rows": with_transposed(L1_cond_weights),
        "w2_rows": a(L2_cond_weights).reshape(-1, C),
        "bias_t": a(fside_8xS_0).T,
        "w_all": np.concatenate(
            [by_block(L3_cond_Wg), by_block(L3_cond_Wu), a(L3_cond_Wd).reshape(BLOCKS, P, T),
             a(L3_cond_Ad).reshape(ADAPTERS, BLOCKS, P, RANK).transpose(1, 2, 0, 3).reshape(BLOCKS, P, P)],
            axis=2),
        "a_all": np.concatenate([adapters_in(L3_cond_Ag), adapters_in(L3_cond_Au)], axis=1),
        "b_rows": np.concatenate([adapters_out(L3_cond_Bg), adapters_out(L3_cond_Bu)], axis=2).reshape(P, -1),
        "bd_rows": a(L3_cond_Bd).reshape(P, T),
    }
    arrays = {name: np.ascontiguousarray(v) for name, v in arrays.items()}

    nc = bacc.Bacc("TRN2", target_bir_lowering=False, num_devices=1)
    t = {name: nc.dram_tensor(name, v.shape, mybir.dt.from_np(v.dtype), kind="ExternalInput").ap()
         for name, v in arrays.items()}
    out = nc.dram_tensor("out", (SAMPLES, C, T), F32, kind="ExternalOutput").ap()
    cond_resid_kernel(nc, t["x"], t["subject"], t["adapter"], t["w0_rows"], t["w1_rows"], t["w2_rows"],
                      t["bias_t"], t["w_all"], t["a_all"], t["b_rows"], t["bd_rows"], out)
    r = run_bass_kernel_spmd(nc, [arrays], core_ids=[0])
    return r.results[0]["out"]
```
